# Optimizing a Trainium2 kernel written in Bass

```python
import numpy as np
import jax
import jax.numpy as jnp

def _softmax(x, axis=-1):
    return jax.nn.softmax(x, axis=axis)

def _gelu(x):
    return jax.nn.gelu(x, approximate=True)

def _silu(x):
    return jax.nn.silu(x)

def _sigmoid(x):
    return jax.nn.sigmoid(x)

def _layernorm(x, axis=-1, eps=1e-05):
    m = jnp.mean(x, axis=axis, keepdims=True)
    v = jnp.var(x, axis=axis, keepdims=True)
    return (x - m) / jnp.sqrt(v + eps)

def _scatter_add(tgt, idx, src, axis=0):
    return tgt.at[idx].add(src)

def _segment_sum(src, seg, n):
    return jax.ops.segment_sum(src, seg, n)
kernel_name = 'mk_gnn_resnorm_d2_gnn_r32_375d34'

def setup_inputs(seed: int=0):
    np.random.seed(seed)
    _w = jnp.asarray

    def _rec_inputs():
        import jax
        import jax.numpy as jnp
        _gk = jax.random.key(seed)
        x = -0.0003713 + 1 * jax.random.normal(jax.random.fold_in(_gk, 1), (3125, 256), jnp.float32)
        _s = jax.random.randint(jax.random.fold_in(_gk, 2), (25000,), 0, 3125, jnp.int32)
        _d = jax.random.randint(jax.random.fold_in(_gk, 3), (25000,), 0, 3125, jnp.int32)
        _loop = jnp.arange(3125, dtype=jnp.int32)
        src = jnp.concatenate([_s, _d, _loop])
        dst = jnp.concatenate([_d, _s, _loop])
        _o = jnp.argsort(dst, stable=True)
        src = src[_o]
        dst = dst[_o]
        edge_weight = -0.000423496 + 0.100023 * jax.random.normal(jax.random.fold_in(_gk, 12), (53125,), jnp.float32)
        return (x, src, dst, edge_weight)
    x, src, dst, edge_weight = _rec_inputs()

    def _L0_gnn_setup():
        import jax, jax.numpy as jnp
        import numpy as np
        N_NODES = 50000
        N_EDGES = 25000
        D = 256
        L = 3
        key = jax.random.key(seed)
        k1, k2, k3, k4, k5 = jax.random.split(key, 5)
        features = jax.random.normal(k1, (N_NODES, D), dtype=jnp.float32)
        scale = 1.0 / np.sqrt(D)
        W_self = jax.random.normal(k2, (L, D, D), dtype=jnp.float32) * scale
        W_neigh = jax.random.normal(k3, (L, D, D), dtype=jnp.float32) * scale
        bias = jnp.zeros((L, D), dtype=jnp.float32)
        src = jax.random.randint(k4, (N_EDGES,), 0, N_NODES, dtype=jnp.int32)
        dst = jax.random.randint(k5, (N_EDGES,), 0, N_NODES, dtype=jnp.int32)
        return {'features': features, 'W_self': W_self, 'W_neigh': W_neigh, 'bias': bias, 'src': src, 'dst': dst}
    _L0_gnn_all = _L0_gnn_setup()
    _L0_gnn_in = {k: v for k, v in _L0_gnn_all.items() if k in ('W_self', 'W_neigh', 'bias')}
    del _L0_gnn_all

    def _L1_gnn_setup():
        import jax, jax.numpy as jnp
        import numpy as np
        BLOCK_DIMS = [8] * 32

        def _mask_indices():
            d = sum(BLOCK_DIMS)
            mask = np.ones((d, d), dtype=np.int8)
            off = 0
            for b in BLOCK_DIMS:
                mask[off:off + b, off:off + b] = 0
                off += b
            rows, cols = np.nonzero(mask)
            return (d, rows.astype(np.int32), cols.astype(np.int32))
        key = jax.random.key(seed)
        k1, k2 = jax.random.split(key)
        d, rows, cols = _mask_indices()
        N = 15625
        X = jax.random.normal(k1, (N, d), dtype=jnp.float32)
        w_est = 0.1 * jax.random.normal(k2, (rows.shape[0],), dtype=jnp.float32)
        return {'X': X, 'w_est': w_est, 'rows': jnp.asarray(rows), 'cols': jnp.asarray(cols)}
    _L1_gnn_all = _L1_gnn_setup()
    _L1_gnn_in = {k: v for k, v in _L1_gnn_all.items() if k in ()}
    del _L1_gnn_all
    return {'x': x, 'src': src, 'dst': dst, 'edge_weight': edge_weight, 'L0_gnn_W_self': _L0_gnn_in['W_self'], 'L0_gnn_W_neigh': _L0_gnn_in['W_neigh'], 'L0_gnn_bias': _L0_gnn_in['bias']}

def reference(x, src, dst, edge_weight, L0_gnn_W_self, L0_gnn_W_neigh, L0_gnn_bias):
    import jax
    import jax.numpy as jnp

    def _L0_gnn_ref(features, W_self, W_neigh, bias, src, dst):
        import jax, jax.numpy as jnp
        import numpy as np
        N_NODES = 50000
        N_EDGES = 25000
        D = 256
        L = 3
        "3-layer GraphSAGE encoder (DGL SAGEConv, mean aggregator), eval mode.\n\n            Per layer: h_neigh = mean over in-neighbors of h (messages src -> dst);\n                       out = h @ W_self + h_neigh @ W_neigh + bias; relu except last.\n            feat_drop / wrapper dropout are identity in eval mode. The wrapper's relu\n            after layers 0,1 is idempotent with SAGEConv's internal relu.\n            "
        n = features.shape[0]
        ones = jnp.ones(src.shape[0], dtype=features.dtype)
        deg = jax.ops.segment_sum(ones, dst, num_segments=n)
        inv_deg = jnp.where(deg > 0, 1.0 / jnp.maximum(deg, 1.0), 0.0)[:, None]
        h = features
        for l in range(L):
            agg = jax.ops.segment_sum(h[src], dst, num_segments=n) * inv_deg
            h = h @ W_self[l] + agg @ W_neigh[l] + bias[l]
            if l < L - 1:
                h = jax.nn.relu(h)
        return h

    def _L1_gnn_ref(X, w_est, rows, cols):
        import jax, jax.numpy as jnp
        import numpy as np
        BLOCK_DIMS = [8] * 32

        def _mask_indices():
            d = sum(BLOCK_DIMS)
            mask = np.ones((d, d), dtype=np.int8)
            off = 0
            for b in BLOCK_DIMS:
                mask[off:off + b, off:off + b] = 0
                off += b
            rows, cols = np.nonzero(mask)
            return (d, rows.astype(np.int32), cols.astype(np.int32))
        d = X.shape[1]
        W = jnp.zeros((d, d), dtype=X.dtype).at[rows, cols].set(w_est)
        return X @ W
    x = _layernorm(x + _L0_gnn_ref(x, L0_gnn_W_self, L0_gnn_W_neigh, L0_gnn_bias, src, dst), axis=-1)
    x = _layernorm(x + _L1_gnn_ref(x, edge_weight, src, dst), axis=-1)
    return x

_drawn_inputs = setup_inputs


def setup_inputs(seed=0):
    import zlib

    import numpy as np

    out = dict(_drawn_inputs(seed))
    spreads = {'L0_gnn_bias': (0.0, 0.1)}
    factors = {}
    for name, (base, spread) in spreads.items():
        noise = np.random.default_rng([zlib.crc32(name.encode()), seed]).standard_normal(out[name].shape)
        drawn = base * np.exp(spread * noise) if base else spread * noise
        out[name] = jnp.asarray(drawn.astype(out[name].dtype))
    for name, factor in factors.items():
        out[name] = (out[name] * factor).astype(out[name].dtype)
    return out
```

```python
from contextlib import ExitStack

import concourse.bass as bass
from concourse import mybir

ALU = mybir.AluOpType
ACT = mybir.ActivationFunctionType
AX = mybir.AxisListType
F32 = mybir.dt.float32
F16 = mybir.dt.float16
I32 = mybir.dt.int32

N = 3125
D = 256
E = 53125
LAYERS = 3
NP = 125
NT = N // NP
G5 = 5
NG = N // G5
GT = NG // NT
WIN = 128
ROWS = E // NP
KT = D // 128
LO = 2048.0
CHUNKS = (8, 8, 9)
BANKS = ((4, 4), (4, 4), (4, 4, 1))
NC_ROW = G5 * len(CHUNKS)
NB_TILE = sum(len(b) for b in BANKS)
NB_ROW = G5 * NB_TILE
GW = 52
EPS = 1e-5
MAGIC = 12582912.0
HI_MAX = 60000.0
SLOTS = 3


def before(v, period, slots):
    if v >= slots:
        return v - slots
    last = (period - 1) - ((period - 1 - v) % slots)
    return last - period


def after(engine, sem, count):
    if isinstance(count, int) and count <= 0:
        return
    engine.wait_ge(sem, count)


class Steps:

    def __init__(self, engine, sem):
        self.engine, self.sem, self.base, self.start, self.k = engine, sem, 0, 0, 0

    def row(self, j, per):
        self.start, self.k = self.base + per * j, 0

    def end_rows(self, per):
        assert self.k == per, (self.k, per)
        self.base += G5 * per
        self.start, self.k = self.base, 0

    def __call__(self, instruction):
        instruction.then_inc(self.sem, 1)
        self.k += 1
        self.engine.wait_ge(self.sem, self.start + self.k)

    def done(self):
        self.base += self.k
        self.start, self.k = self.base, 0


def build(nc, x, pairs, dst, heads, ew, w_self, w_neigh, bias, bias_cols, out, feat_t):
    with ExitStack() as ctx:
        def sb(name, shape, dt):
            return ctx.enter_context(nc.sbuf_tensor(name, shape, dt))

        def ps(name, shape):
            return ctx.enter_context(nc.psum_tensor(name, shape, F32))

        def sem(name):
            return ctx.enter_context(nc.semaphore(name))

        counts_mem = sb("counts", [NP, NT * G5 * NG + 1], F16)
        counts = counts_mem[:, 0:NT * G5 * NG].rearrange("p (a g) -> p a g", g=NG)
        messages = sb("messages", [NP, NT, 2 * D], F16)
        hot_mem = sb("hot", [128, 4 * NP * 9], F16)
        hot = hot_mem[:, :].rearrange("p (r s n) -> p r s n", r=2, s=2)
        early = sb("early", [128, NP * 9 + 2 * NG + 1], F16)
        feat_in = sb("feat_in", [128, SLOTS, D], F32)
        feat_out = sb("feat_out", [128, SLOTS, D], F32)
        wn = sb("wn", [128, KT, D], F32)
        ws = sb("ws", [128, KT, D], F32)
        ident = sb("ident", [128, 128], F32)
        bias_t = sb("bias_t", [128, LAYERS, KT], F32)
        win_w = sb("win_w", [NP, WIN], F32)
        win_s = sb("win_s", [NP, WIN], F32)
        win_j = sb("win_j", [NP, WIN], F32)
        rest = sb("rest", [NP, 2, D], F32)
        degree = sb("degree", [NP, NT], F32)
        inv_deg = sb("inv_deg", [NP, NT], F32)
        square = sb("square", [NP, D], F32)
        squares = sb("squares", [NP, D], F32)
        small = sb("small", [NP, 64], F32)

        ramp9 = early[:, 0:NP * 9].rearrange("p (v n) -> p v n", n=9)
        key_src = early[:, NP * 9:NP * 9 + NG]
        key_dst = early[:, NP * 9 + NG:NP * 9 + 2 * NG]
        late = early[:, :].bitcast(F32)
        w1 = late[:, 0:KT * D].rearrange("p (k n) -> p k n", k=KT)
        bias_row = late[0:NP, KT * D:KT * D + D]
        ramp_d = late[:, 768:768 + D]
        slot_no = late[0:GW, 1024:1024 + WIN]

        tmp, tmp_i = counts_mem[:, :].bitcast(F32), counts_mem[:, :].bitcast(I32)

        def area(base, k, n, view=tmp):
            return view[:, base:base + k * n].rearrange("p (k n) -> p k n", k=k)
        rows_a, rows_b = tmp_i[:, 0:ROWS], tmp_i[:, 512:512 + ROWS]
        heads_i, heads_f = tmp_i[:, 1024:1024 + ROWS], tmp[:, 1536:1536 + ROWS]
        junk = tmp[:, 2048:2048 + ROWS]
        found_i, found_f = area(2560, 5, NP, tmp_i), area(3200, 5, NP)
        win_flat = area(4096, 5, 2 * WIN, tmp_i)
        win = win_flat.rearrange("p k (n two) -> p k n two", two=2)
        src, jd = area(5632, 5, WIN), area(6272, 5, WIN)
        va, vb, vc, vd = (area(7168 + 640 * q, 5, WIN) for q in range(4))
        f_dst, f_src = area(9728, 5, WIN), area(10368, 5, WIN)
        thr_i, thr = tmp_i[:, 11008:11013], tmp[:, 11016:11021]
        cnt, fine, head_row = tmp[:, 11024:11029], tmp[:, 11032:11037], tmp[:, 11040:11045]
        row_i, start_i = tmp_i[:, 11048:11053], tmp_i[:, 11056:11061]

        work = hot_mem[:, :].bitcast(F32)
        agg_sb = work[0:NP, 0:2 * D].rearrange("p (r f) -> p r f", r=2)
        h_sb = work[0:NP, 512:512 + 2 * D].rearrange("p (r f) -> p r f", r=2)
        same = work[0:GW, 1024:1024 + 5 * WIN].rearrange("p (i n) -> p i n", n=WIN)
        win_k, last = work[0:GW, 1664:1664 + WIN], work[0:GW, 1792:1792 + WIN]
        factor = work[:, 1024:1024 + 2 * D].rearrange("p (r f) -> p r f", r=2)
        turned = work[:, 1536:1536 + 3 * GW].rearrange("p (q g) -> p q g", q=3)
        hot_j = work[:, 1696:1696 + 5 * GW].rearrange("p (g j) -> p g j", j=5)
        ut_sb = work[:, 1024:1024 + 2 * D].rearrange("p (r k n) -> p r k n", r=2, k=KT)[:, :, :, 0:NP]
        res_sb = work[0:NP, 1536:1536 + 2 * D].rearrange("p (r f) -> p r f", r=2)

        agg = [ps(f"agg{q}", [128, 512]) for q in range(3)]
        own = [ps(f"own{q}", [128, 512]) for q in range(2)]
        turn = [ps(f"turn{q}", [128, 512]) for q in range(2)]
        mix = ps("mix", [128, 512])
        built = agg + [mix]

        rows_in, heads_in = sem("rows_in"), sem("heads_in")
        found_in, win_in, win_w_in = sem("found_in"), sem("win_in"), sem("win_w_in")
        bias_in, bias_row_in, wn_in, ws_in = sem("bias_in"), sem("bias_row_in"), sem("wn_in"), sem("ws_in")
        feat_loaded = [sem(f"feat_loaded{q}") for q in range(SLOTS)]
        feat_stored = [sem(f"feat_stored{q}") for q in range(SLOTS)]
        x_loaded = [sem(f"x_loaded{q}") for q in range(SLOTS)]
        out_stored = [sem(f"out_stored{q}") for q in range(2)]
        constants, pool_step = sem("constants"), sem("pool_step")
        rows_at, windows_at = sem("rows_at"), sem("windows_at")
        dve_step, keys_ok, keys_turned, act_step = sem("dve_step"), sem("keys_ok"), sem("keys_turned"), sem("act_step")
        keys_kept = sem("keys_kept")
        hot_ok, summed, kept = sem("hot_ok"), sem("summed"), sem("kept")
        xt_kept, feat_read = sem("xt_kept"), sem("feat_read")
        msg_ok, hi_ok, rest_ok, lo_ok = sem("msg_ok"), sem("hi_ok"), sem("rest_ok"), sem("lo_ok")
        range_seen = sem("range_seen")
        agg_ok, h_ok = sem("agg_ok"), sem("h_ok")
        h_turned, ht_kept = sem("h_turned"), sem("ht_kept")
        late_ok, edges_ok, edges_turned, factor_ok, scattered, w1_ok = (
            sem("late_ok"), sem("edges_ok"), sem("edges_turned"), sem("factor_ok"), sem("scattered"), sem("w1_ok"))
        xb_ok, var_ok, root_ok, mixed, out_ok = (
            sem("xb_ok"), sem("var_ok"), sem("root_ok"), sem("mixed"), sem("out_ok"))
        var2_ok, root2_ok, res_ok = sem("var2_ok"), sem("root2_ok"), sem("res_ok")

        x_tiles = x.rearrange("(t p j) f -> t p j f", t=G5, p=NP)
        out_tiles = out.rearrange("(t p j) f -> t p j f", t=G5, p=NP)
        self_w = w_self.rearrange("l (k p) n -> l p k n", p=128)
        neigh_w = w_neigh.rearrange("l (k p) n -> l p k n", p=128)

        def in_slot(q):
            return feat_in[:, q, 0:KT * NP].rearrange("p (k n) -> p k n", k=KT)

        def out_slot(q):
            return feat_out[:, q, 0:KT * NP].rearrange("p (k n) -> p k n", k=KT)

        per_row = [len([b for b in range(G5) if b % SLOTS == q]) for q in range(SLOTS)]

        def nth(n, j, b):
            if b < 0:
                j, b = j - 1, b + G5
            return per_row[b % SLOTS] * (G5 * n + j) + b // SLOTS + 1

        def rows(engine, body):
            body(0)
            with engine.Fori(1, G5) as j:
                body(j)

        block = ctx.enter_context(nc.Block())

        @block.sync
        def _(sp):
            sp.dma_start(heads_i, heads.rearrange("(a r) -> a r", a=1).broadcast_to([NP, ROWS])
                         ).then_inc(heads_in, 16)
            sp.dma_start(bias_t[:, :, :], bias_cols).then_inc(bias_in, 16)
            sp.dma_start(wn[:, :, :], neigh_w[0]).then_inc(wn_in, 16)
            sp.dma_start(ws[:, :, :], self_w[0]).then_inc(ws_in, 16)

            def load_x(j):
                for b in range(G5):
                    after(sp, feat_read, G5 * j + before(b, G5, SLOTS) + 1)
                    sp.dma_start(feat_in[0:NP, b % SLOTS, :], x_tiles[b, :, j, :]
                                 ).then_inc(feat_loaded[b % SLOTS], 16)
            for j in range(G5):
                load_x(j)

            def load_features(layer, n, fresh):
                def load(j):
                    if fresh:
                        for q in range(SLOTS):
                            sp.wait_ge(feat_stored[q], 16 * per_row[q] * (G5 * layer + j + 1))
                    for b in range(G5):
                        sp.wait_ge(feat_read, NT * n + G5 * j + before(b, G5, SLOTS) + 1)
                        sp.dma_start(feat_in[:, b % SLOTS, 0:KT * NP], feat_t[layer, G5 * j + b]
                                     ).then_inc(feat_loaded[b % SLOTS], 16)
                        if n == 5:
                            if j == 0 and b < SLOTS:
                                sp.wait_ge(feat_stored[b], 16 * per_row[b] * G5 * LAYERS)
                            after(sp, h_ok, 2 * NT + G5 * j + before(b, G5, SLOTS) + 1)
                            sp.dma_start(feat_out[0:NP, b % SLOTS, :], x_tiles[b, :, j, :]
                                         ).then_inc(x_loaded[b % SLOTS], 16)
                for j in range(G5):
                    load(j)

            for layer in range(LAYERS):
                if layer:
                    load_features(layer, 2 * layer, True)
                    sp.wait_ge(feat_read, 2 * NT * layer)
                    sp.dma_start(ws[:, :, :], self_w[layer]).then_inc(ws_in, 16)
                load_features(layer, 2 * layer + 1, layer == 0)
                if layer + 1 < LAYERS:
                    sp.wait_ge(feat_read if layer else msg_ok, NT * (2 * layer + 1))
                    sp.dma_start(wn[:, :, :], neigh_w[layer + 1]).then_inc(wn_in, 16)

        @block.gpsimd
        def _(pool):
            nc.gpsimd.memset(ident[:, :], 0.0).then_inc(pool_step, 1)
            nc.gpsimd.iota(thr_i, pattern=[[NG, 5]], base=0, channel_multiplier=G5).then_inc(constants, 1)
            nc.gpsimd.iota(ramp9, pattern=[[1, NP], [0, 9]], base=0, channel_multiplier=0,
                           allow_small_or_imprecise_dtypes=True).then_inc(constants, 1)
            pool.wait_ge(pool_step, 1)
            nc.gpsimd.affine_select(out=ident[:, :], in_=ident[:, :], compare_op=ALU.not_equal, fill=1.0,
                                    base=0, pattern=[[-1, 128]], channel_multiplier=1).then_inc(constants, 1)
            nc.gpsimd.memset(squares[:, :], 0.0).then_inc(range_seen, 1)
            nc.gpsimd.memset(square[:, :], 0.0).then_inc(range_seen, 1)

            pool.wait_ge(rows_at, 1)
            for t in range(5):
                nc.gpsimd.indirect_dma_start(
                    out=found_i[:, t, :], out_offset=None, in_=dst[0:E].rearrange("(r n) -> r n", n=NP),
                    in_offset=bass.IndirectOffsetOnAxis(ap=row_i[:, t:t + 1], axis=0),
                    bounds_check=ROWS - 1, oob_is_err=False).then_inc(found_in, 16)
            pool.wait_ge(windows_at, 1)
            for t in range(5):
                nc.gpsimd.indirect_dma_start(
                    out=win_flat[:, t, :], out_offset=None, in_=pairs,
                    in_offset=bass.IndirectOffsetOnAxis(ap=start_i[:, t:t + 1], axis=0),
                    bounds_check=E, oob_is_err=False).then_inc(win_in, 16)
            nc.gpsimd.indirect_dma_start(
                out=win_w[:, :], out_offset=None, in_=ew.rearrange("(n a) -> n a", a=1),
                in_offset=bass.IndirectOffsetOnAxis(ap=start_i[:, 0:1], axis=0),
                bounds_check=E, oob_is_err=False).then_inc(win_w_in, 16)

            def see_range(layer):
                def row(j):
                    for b in range(G5):
                        at = 2 * (NT * layer + G5 * j + b)
                        pool.wait_ge(hi_ok, NT * layer + G5 * j + b + 1)
                        pool.wait_ge(range_seen, at + 2)
                        tile = messages[:, G5 * j + b, 0:D]
                        nc.gpsimd.tensor_tensor(square[:, :], tile, tile, ALU.mult).then_inc(range_seen, 1)
                        pool.wait_ge(range_seen, at + 3)
                        nc.gpsimd.tensor_tensor(squares[:, :], squares[:, :], square[:, :], ALU.add
                                                ).then_inc(range_seen, 1)
                rows(pool, row)

            see_range(0)
            pool.wait_ge(hot_ok, NC_ROW * G5)
            nc.gpsimd.iota(slot_no, pattern=[[1, WIN]], base=1, channel_multiplier=0,
                           allow_small_or_imprecise_dtypes=True).then_inc(late_ok, 1)
            nc.gpsimd.iota(ramp_d, pattern=[[1, D]], base=0, channel_multiplier=0,
                           allow_small_or_imprecise_dtypes=True).then_inc(late_ok, 1)
            pool.dma_start(bias_row, bias[LAYERS - 1:LAYERS, :].broadcast_to([NP, D])).then_inc(bias_row_in, 16)
            see_range(1)
            see_range(2)

            pool.wait_ge(bias_row_in, 16)

            def store_out(j, b):
                j, b = (j - 1, b + G5) if b < 0 else (j, b)
                pool.wait_ge(res_ok, G5 * j + b + 1)
                pool.dma_start(out_tiles[b, :, j, :], res_sb[:, b % 2, :]).then_inc(out_stored[b % 2], 16)

            def add_bias(j):
                for b in range(G5):
                    q = b % SLOTS
                    pool.wait_ge(x_loaded[q], 16 * nth(0, j, b))
                    nc.gpsimd.tensor_tensor(feat_out[0:NP, q, :], feat_out[0:NP, q, :], bias_row,
                                            ALU.add).then_inc(xb_ok, 1)
                    if not (isinstance(j, int) and b == 0):
                        store_out(j, b - 1)
            rows(pool, add_bias)
            store_out(G5, -1)
            pool.wait_ge(out_stored[0], 16 * 15)
            pool.wait_ge(out_stored[1], 16 * 10)

        @block.tensor
        def _(pe):
            pe.wait_ge(constants, 3)
            pe.wait_ge(keys_ok, 1)
            for bank, keys in ((own, vc), (turn, vd)):
                for t in range(5):
                    to = bank[t // 4][:, WIN * (t % 4):WIN * (t % 4) + NP]
                    ins = nc.tensor.transpose(to, keys[:, t, :], ident[0:NP, 0:NP])
            ins.then_inc(keys_turned, 1)
            pe.wait_ge(keys_kept, 4)

            def build_row(j):
                for b in range(G5):
                    tile = G5 * j + b

                    def turn_x():
                        pe.wait_ge(feat_loaded[b % SLOTS], 16 * nth(0, j, b))
                        after(pe, xt_kept, G5 * j + before(b, G5, 2) + 1)
                        for k in range(KT):
                            ins = nc.tensor.transpose(turn[b % 2][:, k * NP:(k + 1) * NP],
                                                      feat_in[0:NP, b % SLOTS, k * 128:(k + 1) * 128],
                                                      ident[0:NP, 0:NP])
                        ins.then_inc(feat_read, 1)

                    def message():
                        if b == 0 and isinstance(j, int):
                            pe.wait_ge(wn_in, 16)
                        pe.wait_ge(xt_kept, tile + 1)
                        after(pe, rest_ok, G5 * j + before(b, G5, 2) + 1)
                        for k in range(KT):
                            ins = nc.tensor.matmul(own[b % 2][0:NP, 0:D], out_slot(b % SLOTS)[:, k, :],
                                                   wn[:, k, :], start=(k == 0), stop=(k == KT - 1))
                        ins.then_inc(msg_ok, 1)

                    turn_x()
                    u = b * NB_TILE
                    for c, n in enumerate(CHUNKS):
                        w = b * len(CHUNKS) + c
                        pe.wait_ge(hot_ok, NC_ROW * j + w + 1)
                        one = [hot[:, w % 2, s, 0:NP * n].rearrange("p (v n) -> p v n", n=n) for s in range(2)]
                        g = 0
                        for m in BANKS[c]:
                            after(pe, kept, NB_ROW * j + before(u, NB_ROW, 4) + 1)
                            for q in range(m):
                                ins = nc.tensor.matmul(built[u % 4][0:NP, q * NP:(q + 1) * NP],
                                                       one[0][:, :, g], one[1][:, :, g], start=True, stop=True)
                                g += 1
                            ins.then_inc(summed, 1)
                            u += 1
                        if c == 0:
                            message()
            rows(pe, build_row)

            def aggregate(layer):
                n = 2 * layer + 1

                def turn_h(j, b):
                    t = NT * layer + G5 * j + b
                    pe.wait_ge(h_ok, t + 1)
                    after(pe, ht_kept, t)
                    for k in range(KT):
                        ins = nc.tensor.transpose(turn[0][:, k * NP:(k + 1) * NP],
                                                  h_sb[:, b % G5 % 2, k * 128:(k + 1) * 128], ident[0:NP, 0:NP])
                    ins.then_inc(h_turned, 1)

                def mix_h(j, b):
                    t = G5 * j + b
                    pe.wait_ge(ht_kept, 2 * NT + t + 1)
                    after(pe, out_ok, t)
                    for k in range(KT):
                        ins = nc.tensor.matmul(mix[0:NP, 0:D], ut_sb[:, b % G5 % 2, k, :], w1[:, k, :],
                                               start=(k == 0), stop=(k == KT - 1))
                    ins.then_inc(mixed, 1)

                def scatter(groups, first):
                    for q, g in enumerate(groups):
                        pe.wait_ge(factor_ok, first + q + 1)
                        for k, bank in enumerate((mix, turn[1])):
                            ins = nc.tensor.matmul(bank[:, bass.ds(g * 5, 5)], factor[:, q % 2, k * 128:(k + 1) * 128],
                                                   hot_j[:, g, :], start=True, stop=True)
                        ins.then_inc(scattered, 1)

                def row(j):
                    for b in range(G5):
                        tile = NT * layer + G5 * j + b
                        lagged = not (isinstance(j, int) and b == 0)
                        pe.wait_ge(feat_loaded[b % SLOTS], 16 * nth(n, j, b))
                        after(pe, h_ok, NT * layer + G5 * j + before(b, G5, 2) + 1)
                        for k in range(KT):
                            ins = nc.tensor.matmul(own[b % 2][0:NP, 0:D], in_slot(b % SLOTS)[:, k, :],
                                                   ws[:, k, :], start=(k == 0), stop=(k == KT - 1))
                        ins.then_inc(feat_read, 1)
                        after(pe, h_ok, NT * layer + G5 * j + before(b, G5, 3) + 1)
                        for s in range(NT):
                            ins = nc.tensor.matmul(agg[b % 3][0:NP, :], counts[:, G5 * s + j, b * NP:(b + 1) * NP],
                                                   messages[:, s, :], start=(s == 0), stop=(s == NT - 1))
                            if s == 12 and lagged:
                                turn_h(j, b - 1)
                            if s == 20 and layer == 2 and lagged:
                                mix_h(j, b - 1)
                            if s == 16 and layer == 1:
                                t = G5 * j + b
                                scatter((2 * t, 2 * t + 1), 2 * t)
                        ins.then_inc(agg_ok, 1)

                if layer == 0:
                    pe.wait_ge(kept, NB_ROW * G5)
                pe.wait_ge(ws_in, 16 * (layer + 1))
                pe.wait_ge(lo_ok, NT * (layer + 1))
                rows(pe, row)
                turn_h(G5, -1)
                if layer == 1:
                    scatter((GW - 2, GW - 1), GW - 2)
                if layer == 2:
                    mix_h(G5, -1)

            def messages_of(layer):
                n = 2 * layer
                pe.wait_ge(wn_in, 16 * (layer + 1))
                pe.wait_ge(h_ok, NT * layer)

                def row(j):
                    for b in range(G5):
                        pe.wait_ge(feat_loaded[b % SLOTS], 16 * nth(n, j, b))
                        after(pe, rest_ok, NT * layer + G5 * j + before(b, G5, 2) + 1)
                        for k in range(KT):
                            ins = nc.tensor.matmul(own[b % 2][0:NP, 0:D], in_slot(b % SLOTS)[:, k, :],
                                                   wn[:, k, :], start=(k == 0), stop=(k == KT - 1))
                        ins.then_inc(feat_read, 1)
                rows(pe, row)

            aggregate(0)
            pe.wait_ge(edges_ok, 1)
            for q, window in enumerate((win_w, win_s, win_j)):
                ins = nc.tensor.transpose(turn[1][:, q * GW:(q + 1) * GW], window[0:GW, :], ident[0:GW, 0:GW])
            ins.then_inc(edges_turned, 1)
            messages_of(1)
            aggregate(1)
            messages_of(2)
            pe.wait_ge(w1_ok, 2)
            aggregate(2)

        @block.scalar
        def _(act):
            act.dma_start(rows_a, dst[0:E].rearrange("(p n) -> p n", n=ROWS)).then_inc(rows_in, 16)
            act.dma_start(rows_b, dst[1:E + 1].rearrange("(p n) -> p n", n=ROWS)).then_inc(rows_in, 16)
            act.wait_ge(keys_turned, 1)
            for bank, keys in ((own, key_src), (turn, key_dst)):
                nc.scalar.activation(keys[:, 0:4 * NP].rearrange("p (t g) -> p t g", t=4),
                                     bank[0][:, :].rearrange("p (t g) -> p t g", g=WIN)[:, :, 0:NP],
                                     ACT.Copy).then_inc(keys_kept, 1)
                nc.scalar.activation(keys[:, 4 * NP:NG], bank[1][:, 0:NP], ACT.Copy).then_inc(keys_kept, 1)

            def build_row(j):
                for b in range(G5):
                    tile = G5 * j + b
                    q = b % SLOTS
                    act.wait_ge(feat_read, tile + 1)
                    after(act, feat_stored[q], 16 * (nth(0, j, b) - 1))
                    after(act, msg_ok, G5 * j + before(b, G5, SLOTS) + 1)
                    nc.scalar.activation(feat_out[:, q, 0:KT * NP], turn[b % 2][:, 0:KT * NP],
                                         ACT.Copy).then_inc(xt_kept, 1)
                    u = b * NB_TILE
                    g = b * GT
                    for c in range(len(CHUNKS)):
                        for m in BANKS[c]:
                            act.wait_ge(summed, NB_ROW * j + u + 1)
                            nc.scalar.activation(counts[:, :, bass.ds(j * NP + g, m)],
                                                 built[u % 4][0:NP, 0:m * NP].rearrange("p (m k) -> p k m", m=m),
                                                 ACT.Copy).then_inc(kept, 1)
                            u += 1
                            g += m
                        if c == 0:
                            act.wait_ge(xt_kept, tile + 1)
                            act.dma_start(feat_t[0, tile], feat_out[:, q, 0:KT * NP]).then_inc(feat_stored[q], 16)
                            act.wait_ge(msg_ok, tile + 1)
                            nc.scalar.activation(messages[:, tile, 0:D], own[b % 2][0:NP, 0:D],
                                                 ACT.Copy).then_inc(hi_ok, 1)
            act.wait_ge(win_w_in, 16)
            rows(act, build_row)
            act.wait_ge(bias_in, 16)

            def keep_h(layer):
                def row(j):
                    for b in range(G5):
                        q, t = b % SLOTS, NT * layer + G5 * j + b
                        act.wait_ge(h_turned, t + 1)
                        act.wait_ge(feat_stored[q], 16 * (nth(layer + 1, j, b) - 1))
                        for k in range(KT):
                            ins = nc.scalar.activation(out_slot(q)[:, k, :], turn[0][:, k * NP:(k + 1) * NP], ACT.Relu,
                                                       bias=bias_t[:, layer, k:k + 1])
                        ins.then_inc(ht_kept, 1)
                        act.wait_ge(ht_kept, t + 1)
                        act.dma_start(feat_t[layer + 1, G5 * j + b], feat_out[:, q, 0:KT * NP]
                                      ).then_inc(feat_stored[q], 16)
                rows(act, row)

            def keep_hi(layer):
                act.wait_ge(agg_ok, NT * layer)
                act.wait_ge(range_seen, 2 * NT * layer + 2)

                def row(j):
                    for b in range(G5):
                        act.wait_ge(feat_read, 2 * NT * layer + G5 * j + b + 1)
                        nc.scalar.activation(messages[:, G5 * j + b, 0:D], own[b % 2][0:NP, 0:D],
                                             ACT.Copy).then_inc(hi_ok, 1)
                rows(act, row)

            keep_h(0)
            act.wait_ge(edges_turned, 1)
            nc.scalar.activation(turned, turn[1][:, 0:3 * GW].rearrange("p (q g) -> p q g", q=3),
                                 ACT.Copy).then_inc(act_step, 1)
            keep_hi(1)
            keep_h(1)
            act.wait_ge(scattered, GW)
            for k, bank in enumerate((mix, turn[1])):
                nc.scalar.activation(w1[:, k, :], bank[:, 0:D], ACT.Copy).then_inc(w1_ok, 1)
            keep_hi(2)

            def finish_ut(j, b):
                j, b = (j - 1, b + G5) if b < 0 else (j, b)
                t = G5 * j + b
                act.wait_ge(h_turned, 2 * NT + t + 1)
                after(act, mixed, G5 * j + before(b, G5, 2) + 1)
                nc.scalar.activation(ut_sb[:, b % 2, :, :],
                                     turn[0][:, 0:KT * NP].rearrange("p (k n) -> p k n", k=KT),
                                     ACT.Copy).then_inc(ht_kept, 1)
                act.wait_ge(var2_ok, t + 1)
                nc.scalar.activation(small[:, 20:21], small[:, 19:20], ACT.Sqrt, bias=small[:, 40:41]
                                     ).then_inc(root2_ok, 1)

            def row(j):
                for b in range(G5):
                    if not (isinstance(j, int) and b == 0):
                        finish_ut(j, b - 1)
                    act.wait_ge(var_ok, G5 * j + b + 1)
                    nc.scalar.activation(small[:, 8:9], small[:, 7:8], ACT.Sqrt, bias=small[:, 40:41]
                                         ).then_inc(root_ok, 1)
            rows(act, row)
            finish_ut(G5, -1)

        @block.vector
        def _(dve):
            step = Steps(dve, dve_step)
            v = nc.vector
            dve.wait_ge(constants, 3)
            step(v.tensor_copy(thr, thr_i))
            step(v.memset(small[:, 40:41], EPS))
            dve.wait_ge(heads_in, 16)
            step(v.tensor_copy(heads_f, heads_i))
            for t in range(5):
                step(v.tensor_scalar(junk, heads_f, thr[:, t:t + 1], 0.0, ALU.is_lt, ALU.add,
                                     accum_out=cnt[:, t:t + 1]))
            step(v.tensor_scalar(head_row, cnt, 1.0, 0.0, ALU.subtract, ALU.max))
            v.tensor_copy(row_i, head_row).then_inc(rows_at, 1)
            dve.wait_ge(rows_in, 32)
            step(v.tensor_tensor(junk, rows_a, rows_b, ALU.is_gt))
            step(v.tensor_reduce(small[:, 41:42], junk, AX.X, ALU.max))
            dve.wait_ge(found_in, 80)
            step(v.tensor_copy(found_f, found_i))
            for t in range(5):
                step(v.tensor_scalar(junk[:, 0:NP], found_f[:, t, :], thr[:, t:t + 1], 0.0, ALU.is_lt, ALU.add,
                                     accum_out=fine[:, t:t + 1]))
            step(v.scalar_tensor_tensor(out=head_row, in0=head_row, scalar=float(NP), in1=fine,
                                        op0=ALU.mult, op1=ALU.add))
            v.tensor_copy(start_i, head_row).then_inc(windows_at, 1)
            dve.wait_ge(win_in, 80)
            step(v.tensor_copy(f_src, win[:, :, :, 1]))
            step(v.tensor_copy(f_dst, win[:, :, :, 0]))
            for t in range(5):
                step(v.tensor_scalar(jd[:, t, :], f_dst[:, t, :], thr[:, t:t + 1], None, ALU.subtract))
            step(v.tensor_scalar(va, jd, 0.0, None, ALU.is_ge))
            step(v.scalar_tensor_tensor(out=va, in0=jd, scalar=4.0, in1=va, op0=ALU.is_le, op1=ALU.mult))
            step(v.tensor_scalar(vb, f_src, 1.0 / NG, -0.4992, ALU.mult, ALU.add))
            step(v.tensor_scalar(vb, vb, MAGIC, None, ALU.add))
            step(v.tensor_scalar(vb, vb, MAGIC, None, ALU.subtract))
            step(v.scalar_tensor_tensor(out=src, in0=vb, scalar=-float(NG), in1=f_src, op0=ALU.mult, op1=ALU.add))
            step(v.tensor_scalar(vc, src, 1.0 / G5, -0.4, ALU.mult, ALU.add))
            step(v.tensor_scalar(vc, vc, MAGIC, None, ALU.add))
            step(v.tensor_scalar(vc, vc, MAGIC, None, ALU.subtract))
            step(v.scalar_tensor_tensor(out=vd, in0=vc, scalar=-float(G5), in1=src, op0=ALU.mult, op1=ALU.add))
            step(v.scalar_tensor_tensor(out=vd, in0=vd, scalar=25.0, in1=jd, op0=ALU.mult, op1=ALU.add))
            step(v.scalar_tensor_tensor(out=vd, in0=vb, scalar=5.0, in1=vd, op0=ALU.mult, op1=ALU.add))
            step(v.scalar_tensor_tensor(out=vd, in0=vd, scalar=1.0, in1=va, op0=ALU.add, op1=ALU.mult))
            v.tensor_scalar(vd, vd, 1.0, None, ALU.subtract).then_inc(keys_ok, 1)
            for j in range(G5):
                for t in range(5):
                    step(v.tensor_scalar(junk[:, 0:WIN], jd[:, t, :], float(j), 0.0, ALU.is_equal, ALU.add,
                                         accum_out=degree[:, G5 * j + t:G5 * j + t + 1]))
            step(v.tensor_copy(win_s[:, :], f_src[:, 0, :]))
            step(v.scalar_tensor_tensor(out=win_j[:, :], in0=jd[:, 0, :], scalar=1.0, in1=va[:, 0, :],
                                        op0=ALU.add, op1=ALU.mult))
            step(v.tensor_scalar(win_j[:, :], win_j[:, :], 1.0, None, ALU.subtract))
            step(v.tensor_scalar(inv_deg[:, :], degree[:, :], 1.0, None, ALU.max))
            step(v.reciprocal(inv_deg[:, :], inv_deg[:, :]))
            step(v.scalar_tensor_tensor(out=inv_deg[:, :], in0=degree[:, :], scalar=0.0, in1=inv_deg[:, :],
                                        op0=ALU.is_gt, op1=ALU.mult))
            step.done()
            dve.wait_ge(keys_kept, 4)

            def split(layer, tile, b):
                dve.wait_ge(hi_ok, NT * layer + tile + 1)
                after(dve, lo_ok, NT * layer + tile - b + before(b, G5, 2) + 1)
                v.tensor_tensor(rest[:, b % 2, :], own[b % 2][0:NP, 0:D], messages[:, tile, 0:D],
                                ALU.subtract).then_inc(rest_ok, 1)
                dve.wait_ge(rest_ok, NT * layer + tile + 1)
                v.tensor_scalar(messages[:, tile, D:2 * D], rest[:, b % 2, :], LO, None, ALU.mult).then_inc(lo_ok, 1)

            def build_row(j):
                for b in range(G5):
                    g = b * GT
                    for c, n in enumerate(CHUNKS):
                        w = b * len(CHUNKS) + c
                        prev = before(w, NC_ROW, 2)
                        banks = sum(len(BANKS[q % 3]) for q in range(prev + 1)) if prev >= 0 else \
                            -sum(len(BANKS[q % 3]) for q in range(prev + 1, 0))
                        after(dve, summed, NB_ROW * j + banks)
                        for s, keys in enumerate((key_src, key_dst)):
                            ins = v.tensor_tensor(
                                hot[:, w % 2, s, 0:NP * n].rearrange("p (v n) -> p v n", n=n), ramp9[:, :, 0:n],
                                keys[:, bass.ds(j * NP + g, n)].unsqueeze(1).broadcast_to([128, NP, n]), ALU.is_equal)
                        ins.then_inc(hot_ok, 1)
                        g += n
                        if c == 1:
                            split(0, G5 * j + b, b)
            rows(dve, build_row)

            def make_h(layer, j, b):
                t = NT * layer + G5 * j + b
                dve.wait_ge(agg_ok, t + 1)
                step(v.tensor_scalar(agg_sb[:, b % 2, :], agg[b % 3][0:NP, D:2 * D], 1.0 / LO, None, ALU.mult))
                step(v.tensor_tensor(agg_sb[:, b % 2, :], agg_sb[:, b % 2, :], agg[b % 3][0:NP, 0:D], ALU.add))
                after(dve, h_turned, NT * layer + G5 * j + before(b, G5, 2) + 1)
                return v.scalar_tensor_tensor(out=h_sb[:, b % 2, :], in0=agg_sb[:, b % 2, :],
                                              scalar=inv_deg[:, bass.ds(G5 * j + b, 1)], in1=own[b % 2][0:NP, 0:D],
                                              op0=ALU.mult, op1=ALU.add)

            def split_rows(layer):
                dve.wait_ge(agg_ok, NT * layer)

                def row(j):
                    for b in range(G5):
                        split(layer, G5 * j + b, b)
                rows(dve, row)

            dve.wait_ge(summed, NB_ROW * G5)
            dve.wait_ge(late_ok, 2)
            step(v.scalar_tensor_tensor(out=win_k, in0=win_s[0:GW, :], scalar=5.0, in1=win_j[0:GW, :],
                                        op0=ALU.mult, op1=ALU.add))
            step(v.tensor_scalar(last, win_j[0:GW, :], 0.0, None, ALU.is_ge))
            step(v.scalar_tensor_tensor(out=win_k, in0=win_k, scalar=1.0, in1=last, op0=ALU.add, op1=ALU.mult))
            step.done()

            def last_use(i, n):
                mine = win_k[:, bass.ds(i, n)].unsqueeze(2).broadcast_to([GW, n, WIN])
                theirs = win_k.unsqueeze(1).broadcast_to([GW, n, WIN])
                step(v.tensor_tensor(same[:, 0:n, :], mine, theirs, ALU.is_equal))
                step(v.tensor_tensor(same[:, 0:n, :], same[:, 0:n, :],
                                     slot_no.unsqueeze(1).broadcast_to([GW, n, WIN]), ALU.mult))
                step(v.tensor_reduce(last[:, bass.ds(i, n)], same[:, 0:n, :], AX.X, ALU.max))

            def row0(j):
                step.row(j, 5 * G5)
                for b in range(G5):
                    make_h(0, j, b).then_inc(h_ok, 1)
                    last_use((G5 * j + b) * 5, 5)
            rows(dve, row0)
            step.end_rows(5 * G5)
            last_use(125, 3)
            step(v.tensor_tensor(last, last, slot_no, ALU.is_equal))
            step(v.scalar_tensor_tensor(out=last, in0=win_k, scalar=0.5, in1=last, op0=ALU.is_gt, op1=ALU.mult))
            step(v.scalar_tensor_tensor(out=last, in0=win_k, scalar=5.0 * D + 0.5, in1=last,
                                        op0=ALU.is_lt, op1=ALU.mult))
            dve.wait_ge(win_w_in, 16)
            v.tensor_tensor(win_w[0:GW, :], win_w[0:GW, :], last, ALU.mult).then_inc(edges_ok, 1)
            split_rows(1)
            dve.wait_ge(act_step, 1)
            for j in range(5):
                ins = v.tensor_scalar(hot_j[:, :, j], turned[:, 2, :], float(j), None, ALU.is_equal)
            step(ins)
            step.done()

            def make_factor(g, q):
                after(dve, scattered, g - 1)
                v.tensor_scalar(factor[:, q, :], ramp_d, turned[:, 1, bass.ds(g, 1)], turned[:, 0, bass.ds(g, 1)],
                                ALU.is_equal, ALU.mult).then_inc(factor_ok, 1)

            def row1(j):
                step.row(j, 2 * G5)
                for b in range(G5):
                    for q in range(2):
                        make_factor(2 * (G5 * j + b) + q, q)
                    make_h(1, j, b).then_inc(h_ok, 1)
            rows(dve, row1)
            step.end_rows(2 * G5)
            for q in range(2):
                make_factor(GW - 2 + q, q)
            split_rows(2)

            def norm(value, at, t, var, root):
                step(v.bn_stats(small[:, at:at + 6], value))
                v.memset(small[:, 60:61], 0.0)
                v.bn_aggr(small[:, at + 6:at + 8], small[:, at:at + 6]).then_inc(var, 1)
                dve.wait_ge(root, t + 1)
                step(v.reciprocal(small[:, at + 9:at + 10], small[:, at + 8:at + 9]))

            def nth2(j, b):
                return (3, 2)[b % 2] * j + b // 2 + 1

            def finish(j, b):
                j, b = (j - 1, b + G5) if b < 0 else (j, b)
                t = G5 * j + b
                r = res_sb[:, b % 2, :]
                dve.wait_ge(mixed, t + 1)
                after(dve, out_stored[b % 2], 16 * (nth2(j, b) - 1))
                v.tensor_tensor(r, h_sb[:, b % 2, :], mix[0:NP, 0:D], ALU.add).then_inc(out_ok, 1)
                dve.wait_ge(out_ok, t + 1)
                norm(r, 12, t, var2_ok, root2_ok)
                v.tensor_scalar(r, r, small[:, 18:19], small[:, 21:22], ALU.subtract, ALU.mult).then_inc(res_ok, 1)

            def row2(j):
                step.row(j, 8 * G5)
                if not isinstance(j, int):
                    step.start = step.start - 2
                for b in range(G5):
                    if not (isinstance(j, int) and b == 0):
                        finish(j, b - 1)
                    t = G5 * j + b
                    step(make_h(2, j, b))
                    z = h_sb[:, b % 2, :]
                    dve.wait_ge(xb_ok, t + 1)
                    step(v.tensor_tensor(z, z, feat_out[0:NP, b % SLOTS, :], ALU.add))
                    norm(z, 0, t, var_ok, root_ok)
                    v.tensor_scalar(z, z, small[:, 6:7], small[:, 9:10], ALU.subtract, ALU.mult).then_inc(h_ok, 1)
            row2(0)
            with dve.Fori(1, G5) as j:
                row2(j)
            step.base, step.k = step.base + 5 * 8 * G5 - 2, 0
            step.start = step.base
            finish(G5, -1)


_OUT = (N, D)


def kernel(x, src, dst, edge_weight, L0_gnn_W_self, L0_gnn_W_neigh, L0_gnn_bias):
    import numpy as np
    import concourse.bacc as bacc
    from concourse.bass_utils import run_bass_kernel_spmd as run

    src, dst, ew = np.asarray(src), np.asarray(dst), np.asarray(edge_weight)
    dst_pad = np.concatenate([dst, np.full(WIN, N, dst.dtype)])
    src_pad = np.concatenate([src, np.zeros(WIN, src.dtype)])
    arrays = {
        "x": np.asarray(x),
        "pairs": np.ascontiguousarray(np.stack([dst_pad, src_pad], 1)),
        "dst": dst_pad,
        "heads": np.ascontiguousarray(dst[::NP]),
        "ew": np.concatenate([ew, np.zeros(WIN, ew.dtype)]),
        "w_self": np.asarray(L0_gnn_W_self),
        "w_neigh": np.asarray(L0_gnn_W_neigh),
        "bias": np.asarray(L0_gnn_bias),
        "bias_cols": np.ascontiguousarray(np.asarray(L0_gnn_bias).reshape(LAYERS, KT, 128).transpose(2, 0, 1)),
    }
    nc = bacc.Bacc("TRN2", target_bir_lowering=False, num_devices=1)
    args = [nc.dram_tensor(k, v.shape, mybir.dt.from_np(v.dtype), kind="ExternalInput").ap()
            for k, v in arrays.items()]
    out = nc.dram_tensor("out", _OUT, F32, kind="ExternalOutput").ap()
    feat_t = nc.dram_tensor("feat_t", (LAYERS, NT, 128, KT * NP), F32, kind="Internal").ap()
    build(nc, *args, out, feat_t)
    return run(nc, [arrays], core_ids=[0]).results[0]["out"]
```

```python
from contextlib import ExitStack

import concourse.bass as bass
from concourse import mybir

ALU = mybir.AluOpType
ACT = mybir.ActivationFunctionType
AX = mybir.AxisListType
F32 = mybir.dt.float32
F16 = mybir.dt.float16
I32 = mybir.dt.int32

N = 3125
D = 256
E = 53125
LAYERS = 3
NP = 125
NT = N // NP
G5 = 5
NG = N // G5
GT = NG // NT
WIN = 128
ROWS = E // NP
KT = D // 128
LO = 2048.0
CHUNKS = (7, 6, 6, 6)
CW = max(CHUNKS)
STARTS = [sum(CHUNKS[:c]) for c in range(len(CHUNKS))]
BANKS = (4, 3, 3, 3, 3, 3, 3, 3)
BANK_STARTS = [sum(BANKS[:u]) for u in range(len(BANKS))]
NB_TILE = len(BANKS)
NB_ROW = G5 * NB_TILE
NC_ROW = G5 * len(CHUNKS)
HEAD = 8
EARLY_BANKS = 2
GW = 56
GS = 7
NL = 9
LW = 15 * NL
EPS = 1e-5
MAGIC = 12582912.0
HI_MAX = 60000.0
SLOTS = 3


def before(v, period, slots):
    if v >= slots:
        return v - slots
    last = (period - 1) - ((period - 1 - v) % slots)
    return last - period


def after(engine, sem, count):
    if isinstance(count, int) and count <= 0:
        return
    engine.wait_ge(sem, count)


class Steps:

    def __init__(self, engine, sem):
        self.engine, self.sem, self.base, self.start, self.k = engine, sem, 0, 0, 0

    def row(self, j, per):
        self.start, self.k = self.base + per * j, 0

    def end_rows(self, per):
        assert self.k == per, (self.k, per)
        self.base += G5 * per
        self.start, self.k = self.base, 0

    def __call__(self, instruction):
        instruction.then_inc(self.sem, 1)
        self.k += 1
        self.engine.wait_ge(self.sem, self.start + self.k)

    def done(self):
        self.base += self.k
        self.start, self.k = self.base, 0


def build(nc, x, pairs, dst, heads, ew, w_self, w_neigh, bias, bias_cols, out, feat_t, g_feat, g_matrix):
    with ExitStack() as ctx:
        def sb(name, shape, dt):
            return ctx.enter_context(nc.sbuf_tensor(name, shape, dt))

        def ps(name, shape):
            return ctx.enter_context(nc.psum_tensor(name, shape, F32))

        def sem(name):
            return ctx.enter_context(nc.semaphore(name))

        counts_mem_wide = sb("counts", [128, NT * G5 * NG + 1], F16)
        counts_mem = counts_mem_wide[0:NP, :]
        counts = counts_mem[:, 0:NT * G5 * NG].rearrange("p (a g) -> p a g", g=NG)
        messages = sb("messages", [NP, NT, 2 * D], F16)
        hot_mem = sb("hot", [128, 4 * NP * CW], F16)
        hot = hot_mem[:, :].rearrange("p (r s n) -> p r s n", r=2, s=2)
        early = sb("early", [128, 2 * 1088], F16)
        feat_in = sb("feat_in", [128, SLOTS, D], F32)
        feat_out = sb("feat_out", [128, SLOTS, D], F32)
        wn = sb("wn", [128, KT, D], F32)
        ws = sb("ws", [128, KT, D], F32)
        ident = sb("ident", [128, 128], F32)
        bias_t = sb("bias_t", [128, LAYERS, KT], F32)
        win_w = sb("win_w", [NP, WIN], F32)
        win_s = sb("win_s", [NP, WIN], F32)
        win_j = sb("win_j", [NP, WIN], F32)
        rest_t = sb("rest", [128, 2 * D], F32)
        h_sb = sb("h", [NP, 2, D], F32)
        rest = rest_t[0:NP, :].rearrange("p (r f) -> p r f", r=2)
        degree = sb("degree", [NP, NT], F32)
        inv_deg = sb("inv_deg", [NP, NT], F32)
        square = sb("square", [NP, D], F32)
        squares = sb("squares", [NP, D], F32)
        small = sb("small", [NP, 64], F32)
        general = sb("general", [1, 1], I32)

        ramp = early[:, 0:NP * CW].rearrange("p (v n) -> p v n", n=CW)
        key_src = early[:, NP * CW:NP * CW + NG]
        key_dst = early[:, NP * CW + NG:NP * CW + 2 * NG]
        h_16 = h_sb[:, :, :].rearrange("p r f -> p (r f)").bitcast(F16)
        slot_j, no_use = h_16[:, 0:G5 * WIN].rearrange("p (k n) -> p k n", k=G5), h_16[:, 768:768 + WIN]
        late = early[:, :].bitcast(F32)
        w1 = late[:, 0:KT * D].rearrange("p (k n) -> p k n", k=KT)
        bias_row = late[0:NP, KT * D:KT * D + D]
        ramp_d = late[:, 768:768 + D]
        slot_no = early[0:GW, 2048:2048 + WIN]

        tmp, tmp_i = counts_mem[:, :].bitcast(F32), counts_mem[:, :].bitcast(I32)

        def area(base, k, n, view=tmp):
            return view[:, base:base + k * n].rearrange("p (k n) -> p k n", k=k)
        rows_a, rows_b = tmp_i[:, 0:ROWS], tmp_i[:, 512:512 + ROWS]
        heads_i, heads_f = tmp_i[:, 1024:1024 + ROWS], tmp[:, 1536:1536 + ROWS]
        junk = tmp[:, 2048:2048 + ROWS]
        found_i, found_f = area(2560, 5, NP, tmp_i), area(3200, 5, NP)
        win_flat = area(4096, 5, 2 * WIN, tmp_i)
        win = win_flat.rearrange("p k (n two) -> p k n two", two=2)
        src, jd = area(5632, 5, WIN), area(6272, 5, WIN)
        va, vb, vc, vd = (area(7168 + 640 * q, 5, WIN) for q in range(4))
        f_dst, f_src = area(9728, 5, WIN), area(10368, 5, WIN)
        thr_i, thr = tmp_i[:, 11008:11013], tmp[:, 11016:11021]
        cnt, fine, head_row = tmp[:, 11024:11029], tmp[:, 11032:11037], tmp[:, 11040:11045]
        row_i, start_i = tmp_i[:, 11048:11053], tmp_i[:, 11056:11061]
        x_turned = area(11072, G5, KT * NP, counts_mem_wide[:, :].bitcast(F32))
        rest_all = area(12352, NT, D)
        lo_scale = tmp[:, 18752:18752 + D]

        work = hot_mem[:, :].bitcast(F32)
        same = hot_mem[0:GW, 0:NL * WIN].rearrange("p (i n) -> p i n", n=WIN)
        win_k, last = hot_mem[0:GW, 1152:1152 + LW], hot_mem[0:GW, 1288:1288 + LW]
        win_v, win_q = work[0:GW, 712:712 + WIN], work[0:GW, 840:840 + WIN]
        factor = work[:, 712:712 + 2 * D].rearrange("p (q f) -> p q f", q=2)
        turned = work[:, 1224:1224 + 3 * GW].rearrange("p (q g) -> p q g", q=3)
        hot_j = work[:, 1392:1392 + 5 * GW].rearrange("p (g j) -> p g j", j=5)
        ut_sb = work[:, 0:2 * D].rearrange("p (q k n) -> p q k n", q=2, k=KT)[:, :, :, 0:NP]
        res_sb = work[0:NP, 512:512 + 2 * D].rearrange("p (q f) -> p q f", q=2)
        agg_sb = rest

        agg = [ps(f"agg{q}", [128, 512]) for q in range(3)]
        own = [ps(f"own{q}", [128, 512]) for q in range(2)]
        turn = [ps(f"turn{q}", [128, 512]) for q in range(2)]
        mix = ps("mix", [128, 512])
        built = [turn[1], mix]
        msg = [own[1], agg[0], own[0], agg[1]]

        rows_in, heads_in = sem("rows_in"), sem("heads_in")
        found_in, win_in, win_w_in = sem("found_in"), sem("win_in"), sem("win_w_in")
        bias_in, bias_row_in, wn_in, ws_in = sem("bias_in"), sem("bias_row_in"), sem("wn_in"), sem("ws_in")
        feat_loaded = [sem(f"feat_loaded{q}") for q in range(G5)]
        x_turned_stored = [sem(f"x_turned_stored{q}") for q in range(G5)]
        feat_stored = [sem(f"feat_stored{q}") for q in range(SLOTS)]
        x_loaded = [sem(f"x_loaded{q}") for q in range(SLOTS)]
        out_stored = [sem(f"out_stored{q}") for q in range(2)]
        constants, pool_step = sem("constants"), sem("pool_step")
        rows_at, windows_at = sem("rows_at"), sem("windows_at")
        dve_step, keys_ok, keys_turned, act_step = sem("dve_step"), sem("keys_ok"), sem("keys_turned"), sem("act_step")
        keys_kept = sem("keys_kept")
        hot_ok, summed, kept = sem("hot_ok"), sem("summed"), sem("kept")
        xt_kept, feat_read = sem("xt_kept"), sem("feat_read")
        msg_ok, hi_ok, rest_ok, lo_ok = sem("msg_ok"), sem("hi_ok"), sem("rest_ok"), sem("lo_ok")
        range_seen = sem("range_seen")
        agg_ok, h_ok = sem("agg_ok"), sem("h_ok")
        h_turned, ht_kept = sem("h_turned"), sem("ht_kept")
        late_ok, edges_ok, edges_turned, factor_ok, scattered, w1_ok = (
            sem("late_ok"), sem("edges_ok"), sem("edges_turned"), sem("factor_ok"), sem("scattered"), sem("w1_ok"))
        xb_ok, var_ok, root_ok, mixed, out_ok = (
            sem("xb_ok"), sem("var_ok"), sem("root_ok"), sem("mixed"), sem("out_ok"))
        checks_ok, checked, general_ok, special_done = (
            sem("checks_ok"), sem("checked"), sem("general_ok"), sem("special_done"))
        own_read = sem("own_read")
        var2_ok, root2_ok, res_ok = sem("var2_ok"), sem("root2_ok"), sem("res_ok")

        x_tiles = x.rearrange("(r p b) f -> r p b f", r=G5, p=NP)
        out_tiles = out.rearrange("(r p b) f -> r p b f", r=G5, p=NP)
        self_w = w_self.rearrange("l (k p) n -> l p k n", p=128)
        neigh_w = w_neigh.rearrange("l (k p) n -> l p k n", p=128)

        def wide_slot(q):
            return feat_in[:, q, :] if q < SLOTS else feat_out[:, (2, 0)[q - SLOTS], :]

        def halves(slot):
            return slot[:, 0:KT * NP].rearrange("p (k n) -> p k n", k=KT)

        def out_slot(q):
            return feat_out[:, q, 0:KT * NP].rearrange("p (k n) -> p k n", k=KT)

        per_row = [len([b for b in range(G5) if b % SLOTS == q]) for q in range(SLOTS)]

        def nth(n, j, b):
            if b < 0:
                j, b = j - 1, b + G5
            return per_row[b % SLOTS] * (G5 * n + j) + b // SLOTS + 1

        def loaded(n, j, b):
            if n % 2:
                return per_row[b % SLOTS] * (G5 * (n // 2) + j) + b // SLOTS + 1 + G5 * ((n + 1) // 2)
            return (per_row[b] * G5 * (n // 2) if b < SLOTS else 0) + G5 * ((n + 1) // 2) + j + 1

        def rows(engine, body):
            body(0)
            with engine.Fori(1, G5) as j:
                body(j)

        def gen(base, n, view=tmp):
            return view[:, base:base + n]
        g_ramp, g_hot = gen(0, N), gen(3200, N)
        g_sum = area(6400, NT, D + 1)
        g_rows = gen(12900, D + 1)
        g_later, g_keys, g_same = gen(13200, NP), gen(13400, NP), gen(13600, NP)
        g_h, g_mean, g_x, g_st = gen(13800, D), gen(14100, D), gen(14400, D), gen(14700, D)
        g_bias = gen(15000, LAYERS * D)
        g_zero = gen(15800, 512)
        g_t = rest_t[:, 0:4 * NP].rearrange("p (q n) -> p q n", q=4)
        g_c = gen(16400, 32)
        g_pair, g_idx, g_part = gen(16500, 2, tmp_i), gen(16504, 1, tmp_i), gen(16506, 1, tmp_i)
        g_w = gen(16508, 1)
        g_hot_rows, g_step2 = sem("general_rows"), sem("general_place")
        g_carried = sem("general_carried")
        g_names = ("const", "step", "in", "pair", "got", "hot", "sum", "add", "key", "keys_t", "idx", "scat", "zeroed",
                   "tile", "mean", "tr", "kept", "prod", "var", "root", "unit", "st", "stored", "w", "cleared")
        (g_const, g_step, g_in, g_pair_in, g_got, g_hot_ok, g_summed, g_added, g_key_ok, g_keys_t, g_idx_ok, g_scat,
         g_zeroed, g_tile_in, g_mean_ok, g_turned, g_kept, g_prod, g_var, g_root, g_unit, g_st_ok, g_stored, g_w_in,
         g_cleared) = (sem("general_" + n) for n in g_names)

        def if_general(engine, body):
            engine.wait_ge(general_ok, 1)
            flag = engine.value_load(general[0:1, 0:1], min_val=0, max_val=1)
            with engine.If(flag > 0):
                engine.wait_ge(special_done, 1)
                body()

        block = ctx.enter_context(nc.Block())

        @block.sync
        def _(sp):
            sp.dma_start(heads_i, heads.rearrange("(a r) -> a r", a=1).broadcast_to([NP, ROWS])
                         ).then_inc(heads_in, 16)
            sp.dma_start(bias_t[:, :, :], bias_cols).then_inc(bias_in, 16)
            sp.dma_start(wn[:, :, :], neigh_w[0]).then_inc(wn_in, 16)
            sp.dma_start(ws[:, :, :], self_w[0]).then_inc(ws_in, 16)

            def load_x(j):
                for b in range(G5):
                    after(sp, feat_read, G5 * j + b - G5 + 1)
                    sp.dma_start(wide_slot(b)[0:NP, :], x_tiles[j, :, b, :]).then_inc(feat_loaded[b], 16)
            for j in range(G5):
                load_x(j)

            def load_features(layer, n):
                def load(j):
                    if n == 1:
                        for q in range(G5 if j == 0 else 0):
                            sp.wait_ge(x_turned_stored[q], 16 * G5)
                    elif n % 2 == 0:
                        for q in range(SLOTS):
                            sp.wait_ge(feat_stored[q], 16 * per_row[q] * (G5 * (layer - 1) + j + 1))
                    for b in range(G5):
                        q, slot = b % SLOTS, feat_in[:, b % SLOTS, :]
                        if n % 2 == 0:
                            q, slot = b, wide_slot(b)
                            if j > 0:
                                sp.wait_ge(feat_read, NT * n + G5 * (j - 1) + b + 1)
                            elif b < SLOTS:
                                sp.wait_ge(feat_read, NT * n + before(b, G5, SLOTS) + 1)
                            else:
                                out_q = (2, 0)[b - SLOTS]
                                sp.wait_ge(feat_stored[out_q], 16 * per_row[out_q] * G5 * layer)
                        elif j == 0 and b < SLOTS:
                            sp.wait_ge(feat_read, NT * n - G5 + b + 1)
                        else:
                            sp.wait_ge(feat_read, NT * n + G5 * j + before(b, G5, SLOTS) + 1)
                        sp.dma_start(slot[:, 0:KT * NP], feat_t[layer, G5 * j + b]).then_inc(feat_loaded[q], 16)
                        if n == 5:
                            if j == 0 and b < SLOTS:
                                sp.wait_ge(feat_read, NT * n)
                                sp.wait_ge(feat_stored[b], 16 * per_row[b] * G5 * (LAYERS - 1))
                            after(sp, h_ok, 2 * NT + G5 * j + before(b, G5, SLOTS) + 1)
                            sp.dma_start(feat_out[0:NP, b % SLOTS, :], x_tiles[j, :, b, :]
                                         ).then_inc(x_loaded[b % SLOTS], 16)
                for j in range(G5):
                    load(j)

            for layer in range(LAYERS):
                if layer:
                    load_features(layer, 2 * layer)
                    sp.wait_ge(feat_read, 2 * NT * layer)
                    sp.dma_start(ws[:, :, :], self_w[layer]).then_inc(ws_in, 16)
                load_features(layer, 2 * layer + 1)
                if layer + 1 < LAYERS:
                    sp.wait_ge(feat_read if layer else msg_ok, NT * (2 * layer + 1))
                    sp.dma_start(wn[:, :, :], neigh_w[layer + 1]).then_inc(wn_in, 16)


        @block.gpsimd
        def _(pool):
            nc.gpsimd.memset(ident[:, :], 0.0).then_inc(pool_step, 1)
            nc.gpsimd.iota(thr_i, pattern=[[NG, 5]], base=0, channel_multiplier=G5).then_inc(constants, 1)
            nc.gpsimd.iota(ramp, pattern=[[1, NP], [0, CW]], base=0, channel_multiplier=0,
                           allow_small_or_imprecise_dtypes=True).then_inc(constants, 1)
            pool.wait_ge(pool_step, 1)
            nc.gpsimd.affine_select(out=ident[:, :], in_=ident[:, :], compare_op=ALU.not_equal, fill=1.0,
                                    base=0, pattern=[[-1, 128]], channel_multiplier=1).then_inc(constants, 1)
            nc.gpsimd.memset(squares[:, :], 0.0).then_inc(range_seen, 1)
            nc.gpsimd.memset(square[:, :], 0.0).then_inc(range_seen, 1)

            pool.wait_ge(rows_at, 1)
            for t in range(5):
                nc.gpsimd.indirect_dma_start(
                    out=found_i[:, t, :], out_offset=None, in_=dst[0:E].rearrange("(r n) -> r n", n=NP),
                    in_offset=bass.IndirectOffsetOnAxis(ap=row_i[:, t:t + 1], axis=0),
                    bounds_check=ROWS - 1, oob_is_err=False).then_inc(found_in, 16)
            pool.wait_ge(windows_at, 1)
            for t in range(5):
                nc.gpsimd.indirect_dma_start(
                    out=win_flat[:, t, :], out_offset=None, in_=pairs,
                    in_offset=bass.IndirectOffsetOnAxis(ap=start_i[:, t:t + 1], axis=0),
                    bounds_check=E, oob_is_err=False).then_inc(win_in, 16)
            nc.gpsimd.indirect_dma_start(
                out=win_w[:, :], out_offset=None, in_=ew.rearrange("(n a) -> n a", a=1),
                in_offset=bass.IndirectOffsetOnAxis(ap=start_i[:, 0:1], axis=0),
                bounds_check=E, oob_is_err=False).then_inc(win_w_in, 16)

            def see_tile(layer, j, b):
                at = 2 * (NT * layer + G5 * j + b)
                pool.wait_ge(hi_ok, NT * layer + G5 * j + b + 1)
                pool.wait_ge(range_seen, at + 2)
                tile = messages[:, G5 * j + b, 0:D]
                nc.gpsimd.tensor_tensor(square[:, :], tile, tile, ALU.mult).then_inc(range_seen, 1)
                pool.wait_ge(range_seen, at + 3)
                nc.gpsimd.tensor_tensor(squares[:, :], squares[:, :], square[:, :], ALU.add).then_inc(range_seen, 1)

            def see_range(layer):
                def row(j):
                    for b in range(G5):
                        see_tile(layer, j, b)
                rows(pool, row)

            nc.gpsimd.memset(lo_scale, LO).then_inc(pool_step, 1)
            pool.wait_ge(pool_step, 2)
            def low(j):
                for b in range(G5):
                    pool.wait_ge(rest_ok, G5 * j + b + 1)
                    nc.gpsimd.tensor_tensor(messages[:, G5 * j + b, D:2 * D], rest_all[:, G5 * j + b, :], lo_scale,
                                            ALU.mult).then_inc(lo_ok, 1)
            rows(pool, low)
            see_range(0)
            pool.wait_ge(hot_ok, NC_ROW * G5)
            nc.gpsimd.iota(slot_no, pattern=[[1, WIN]], base=1, channel_multiplier=0,
                           allow_small_or_imprecise_dtypes=True).then_inc(late_ok, 1)
            nc.gpsimd.iota(ramp_d, pattern=[[1, D]], base=0, channel_multiplier=0,
                           allow_small_or_imprecise_dtypes=True).then_inc(late_ok, 1)
            pool.dma_start(bias_row, bias[LAYERS - 1:LAYERS, :].broadcast_to([NP, D])).then_inc(bias_row_in, 16)
            see_range(1)

            pool.wait_ge(bias_row_in, 16)

            def store_out(j, b):
                j, b = (j - 1, b + G5) if b < 0 else (j, b)
                pool.wait_ge(res_ok, G5 * j + b + 1)
                pool.dma_start(out_tiles[j, :, b, :], res_sb[:, b % 2, :]).then_inc(out_stored[b % 2], 16)

            def add_bias(j):
                for b in range(G5):
                    q = b % SLOTS
                    pool.wait_ge(x_loaded[q], 16 * nth(0, j, b))
                    nc.gpsimd.tensor_tensor(feat_out[0:NP, q, :], feat_out[0:NP, q, :], bias_row,
                                            ALU.add).then_inc(xb_ok, 1)
                    if not (isinstance(j, int) and b == 0):
                        store_out(j, b - 1)
                    see_tile(2, j, b)
            rows(pool, add_bias)
            store_out(G5, -1)
            pool.wait_ge(out_stored[0], 16 * 15)
            pool.wait_ge(out_stored[1], 16 * 10)
            nc.gpsimd.memset(square[:, :], 0.0).then_inc(special_done, 1)

            def general_path():
                nc.gpsimd.iota(g_ramp, pattern=[[1, N]], base=0, channel_multiplier=0,
                               allow_small_or_imprecise_dtypes=True).then_inc(g_const, 1)
                nc.gpsimd.iota(g_part, pattern=[[0, 1]], base=0, channel_multiplier=1).then_inc(g_const, 1)
                nc.gpsimd.memset(g_zero, 0.0).then_inc(g_zeroed, 1)
                pool.wait_ge(g_zeroed, 1)
                nc.gpsimd.memset(g_rows[:, D:D + 1], 1.0).then_inc(g_const, 1)
                nc.gpsimd.memset(g_c[:, 31:32], 0.0).then_inc(g_carried, 1)
                with pool.Fori(0, ROWS) as r:
                    pool.wait_ge(g_w_in, r * 16 + 16)
                    pool.wait_ge(g_idx_ok, r + 1)
                    pool.wait_ge(g_carried, r + 1)
                    nc.gpsimd.tensor_tensor(g_c[:, 31:32], g_zero[:, 0:1], g_zero[:, 0:1], ALU.add
                                            ).then_inc(g_carried, 1)
                    nc.gpsimd.indirect_dma_start(
                        out=g_matrix, out_offset=bass.IndirectOffsetOnAxis(ap=g_idx[:, 0:1], axis=0),
                        in_=g_w, in_offset=None, bounds_check=D * D - 1, oob_is_err=False).then_inc(g_scat, 16)
                for layer in range(LAYERS):
                    with pool.Fori(0, ROWS) as r:
                        pool.wait_ge(g_got, r + (layer * ROWS + 1))
                        pool.wait_ge(g_carried, r + ((layer + 1) * ROWS + 1))
                        nc.gpsimd.tensor_tensor(g_c[:, 31:32], g_zero[:, 0:1], g_zero[:, 0:1], ALU.add
                                                ).then_inc(g_carried, 1)
                        nc.gpsimd.indirect_dma_start(
                            out=g_rows[:, 0:D], out_offset=None, in_=x if layer == 0 else g_feat[layer - 1],
                            in_offset=bass.IndirectOffsetOnAxis(ap=g_idx[:, 0:1], axis=0),
                            bounds_check=N - 1, oob_is_err=False).then_inc(g_hot_rows, 16)
            if_general(pool, general_path)

        @block.tensor
        def _(pe):
            pe.wait_ge(constants, 3)
            pe.wait_ge(wn_in, 16)

            def first_messages(j):
                def message(j, b):
                    j, b = (j - 1, b + G5) if b < 0 else (j, b)
                    pe.wait_ge(xt_kept, G5 * j + b + 1)
                    after(pe, rest_ok, G5 * j + before(b, G5, 4) + 1)
                    for k in range(KT):
                        ins = nc.tensor.matmul(msg[b % 4][0:NP, 0:D], halves(x_turned[:, b, :])[:, k, :],
                                               wn[:, k, :], start=(k == 0), stop=(k == KT - 1))
                    ins.then_inc(msg_ok, 1)

                for b in range(G5):
                    pe.wait_ge(feat_loaded[b], 16 * loaded(0, j, b))
                    after(pe, xt_kept, G5 * j + before(b, G5, 2) + 1)
                    for k in range(KT):
                        ins = nc.tensor.transpose(turn[b % 2][:, k * NP:(k + 1) * NP],
                                                  wide_slot(b)[0:NP, k * 128:(k + 1) * 128],
                                                  ident[0:NP, 0:NP])
                    ins.then_inc(feat_read, 1)
                    if not (isinstance(j, int) and b == 0):
                        message(j, b - 1)
                return message
            message = first_messages(0)
            with pe.Fori(1, G5) as j:
                first_messages(j)
            message(G5, -1)

            pe.wait_ge(keys_ok, 1)
            pe.wait_ge(rest_ok, NT)
            pe.wait_ge(xt_kept, NT)
            for bank, keys in ((own, vc), (turn, vd)):
                for t in range(5):
                    to = bank[t // 4][:, WIN * (t % 4):WIN * (t % 4) + NP]
                    ins = nc.tensor.transpose(to, keys[:, t, :], ident[0:NP, 0:NP])
            ins.then_inc(keys_turned, 1)
            pe.wait_ge(keys_kept, 4)

            def count(j, b, g):
                k = max(k for k in range(NB_TILE) if BANK_STARTS[k] <= g)
                u, at = b * NB_TILE + k, (g - BANK_STARTS[k]) * NP
                if g in STARTS:
                    pe.wait_ge(hot_ok, NC_ROW * j + b * len(CHUNKS) + STARTS.index(g) + 1)
                if at == 0:
                    after(pe, kept, NB_ROW * j + before(u, NB_ROW, 2) + 1)
                c = max(c for c in range(len(CHUNKS)) if STARTS[c] <= g)
                one = [hot[:, (b * len(CHUNKS) + c) % 2, q, 0:NP * CHUNKS[c]].rearrange(
                    "p (v n) -> p v n", n=CHUNKS[c])[:, :, g - STARTS[c]] for q in range(2)]
                ins = nc.tensor.matmul(built[u % 2][0:NP, at:at + NP], one[0], one[1],
                                       start=True, stop=True)
                if at == (BANKS[k] - 1) * NP:
                    ins.then_inc(summed, 1)

            for b in range(G5):
                for g in range(GT):
                    count(0, b, g)

            def turn_h(layer, j, b):
                t = NT * layer + G5 * j + b
                pe.wait_ge(h_ok, t + 1)
                after(pe, ht_kept, t)
                for k in range(KT):
                    ins = nc.tensor.transpose(turn[0][:, k * NP:(k + 1) * NP],
                                              h_sb[:, b % G5 % 2, k * 128:(k + 1) * 128], ident[0:NP, 0:NP])
                ins.then_inc(h_turned, 1)

            def aggregate(layer):
                n = 2 * layer + 1

                def mix_h(j, b):
                    t = G5 * j + b
                    pe.wait_ge(ht_kept, 2 * NT + t + 1)
                    after(pe, out_ok, t)
                    for k in range(KT):
                        ins = nc.tensor.matmul(mix[0:NP, 0:D], ut_sb[:, b % G5 % 2, k, :], w1[:, k, :],
                                               start=(k == 0), stop=(k == KT - 1))
                    ins.then_inc(mixed, 1)

                def turn_edges():
                    pe.wait_ge(edges_ok, 1)
                    for q, window in enumerate((win_w, win_s, win_j)):
                        ins = nc.tensor.transpose(turn[1][:, q * GW:(q + 1) * GW], window[0:GW, :],
                                                  ident[0:GW, 0:GW])
                    ins.then_inc(edges_turned, 1)

                def scatter(g):
                    pe.wait_ge(factor_ok, g + 1)
                    for k, bank in enumerate((mix, turn[1])):
                        ins = nc.tensor.matmul(bank[:, 5 * g:5 * g + 5], factor[:, g % 2, k * 128:(k + 1) * 128],
                                               hot_j[:, g, :], start=True, stop=True)
                    ins.then_inc(scattered, 1)

                def row(j, build=False, edges=False, scattering=False):
                    for b in range(G5):
                        tile = NT * layer + G5 * j + b
                        lagged = not (isinstance(j, int) and j == 0 and b == 0)
                        read, base = (own_read, 0) if layer == 2 else (h_ok, NT * layer)
                        after(pe, read, base + G5 * j + before(b, G5, 3) + 1)
                        if build:
                            pe.wait_ge(kept, NB_ROW * (j + 1))
                        g = 0
                        for q in range(NT):
                            if not lagged and q in (0, 4):
                                pe.wait_ge(lo_ok, NT * (layer + 1) - (3 if q == 0 else 0))
                            ins = nc.tensor.matmul(agg[b % 3][0:NP, :], counts[:, G5 * q + b, bass.ds(j * NP, NP)],
                                                   messages[:, q, :], start=(q == 0), stop=(q == NT - 1))
                            if q == NT - 1:
                                ins.then_inc(agg_ok, 1)
                            if q == 6:
                                pe.wait_ge(feat_loaded[b % SLOTS], 16 * loaded(n, j, b))
                                after(pe, read, base + G5 * j + before(b, G5, 2) + 1)
                                for k in range(KT):
                                    ins = nc.tensor.matmul(own[b % 2][0:NP, 0:D], halves(feat_in[:, b % SLOTS, :])[:, k, :],
                                                           ws[:, k, :], start=(k == 0), stop=(k == KT - 1))
                                ins.then_inc(feat_read, 1)
                            if q == 12 and lagged:
                                turn_h(layer, j, b - 1)
                            if q == 20 and layer == 2 and lagged:
                                mix_h(j, b - 1)
                            if q == 16 and edges and b == 0:
                                turn_edges()
                            if scattering and q >= 10 and q % 2 == 0 and (q - 10) // 2 < GS and not (j == 3 and b == 0):
                                first = (G5 * (j - 3) + b - 1) * GS
                                if first < GW:
                                    scatter(first + (q - 10) // 2)
                            while build and q >= HEAD and g * (NT - HEAD) < (q - HEAD + 1) * GT:
                                count(j + 1, b, g)
                                g += 1

                pe.wait_ge(ws_in, 16 * (layer + 1))
                if layer == 0:
                    row(0, build=True)
                    with pe.Fori(1, G5 - 1) as j:
                        row(j, build=True)
                    pe.wait_ge(kept, NB_ROW * G5)
                    row(G5 - 1)
                elif layer == 1:
                    row(0)
                    with pe.Fori(1, 3) as j:
                        row(j)
                    row(3, edges=True, scattering=True)
                    row(4, scattering=True)
                else:
                    rows(pe, row)
                if layer == 2:
                    pe.wait_ge(checks_ok, 1)
                    nc.tensor.matmul(turn[1][0:1, 0:2], small[:, 45:46], small[:, 43:45], start=True, stop=True
                                     ).then_inc(checked, 1)
                    turn_h(2, G5, -1)
                    mix_h(G5, -1)

            def messages_of(layer):
                n = 2 * layer
                pe.wait_ge(wn_in, 16 * (layer + 1))

                def row(j):
                    first = isinstance(j, int) and j == 0
                    for b in range(G5):
                        if first and b == 0:
                            pe.wait_ge(h_ok, NT * layer - 1)
                        if first and b == 2:
                            turn_h(layer - 1, G5, -1)
                        pe.wait_ge(feat_loaded[b], 16 * loaded(n, j, b))
                        after(pe, rest_ok, NT * layer + G5 * j + before(b, G5, 4) + 1)
                        for k in range(KT):
                            ins = nc.tensor.matmul(msg[b % 4][0:NP, 0:D], halves(wide_slot(b))[:, k, :],
                                                   wn[:, k, :], start=(k == 0), stop=(k == KT - 1))
                        ins.then_inc(feat_read, 1)
                rows(pe, row)

            aggregate(0)
            messages_of(1)
            aggregate(1)
            messages_of(2)
            pe.wait_ge(w1_ok, 2)
            aggregate(2)

            def general_path():
                pe.wait_ge(g_const, 3)
                with pe.Fori(0, ROWS) as r:
                    pe.wait_ge(g_key_ok, r + 1)
                    nc.tensor.transpose(turn[0][0:NP, 0:NP], g_keys, ident[0:NP, 0:NP]).then_inc(g_keys_t, 1)
                pe.wait_ge(g_in, 32)
                banks = agg + own + turn + [mix]
                for layer in range(LAYERS):
                    with pe.Fori(0, ROWS) as r:
                        pe.wait_ge(g_hot_rows, r * 16 + 16 * (layer * ROWS + 1))
                        pe.wait_ge(g_hot_ok, r + (layer * ROWS + 1))
                        for t in range(NT):
                            if t >= len(banks):
                                pe.wait_ge(g_added, r * NT + (layer * ROWS * NT + t - len(banks) + 1))
                            nc.tensor.matmul(banks[t % len(banks)][0:NP, 0:D + 1], g_hot[:, t * NP:(t + 1) * NP],
                                             g_rows, start=True, stop=True).then_inc(g_summed, 1)
                    pe.wait_ge(g_in, 32 + 32 * (layer + 1))
                    with pe.Fori(0, NT) as t:
                        at = t + (NT * layer + 1)
                        pe.wait_ge(g_tile_in, at * 32)
                        pe.wait_ge(g_mean_ok, at)
                        for q, side in enumerate((g_h, g_mean)):
                            for k in range(KT):
                                ins = nc.tensor.transpose(agg[0][:, (2 * q + k) * NP:(2 * q + k + 1) * NP],
                                                          side[:, k * 128:(k + 1) * 128], ident[0:NP, 0:NP])
                        ins.then_inc(g_turned, 1)
                        pe.wait_ge(g_kept, at if layer < 2 else t * 2 + (2 * NT + 1))
                        for q in range(4):
                            ins = nc.tensor.matmul(own[0][0:NP, 0:D], g_t[:, q, :], (ws, wn)[q // 2][:, q % 2, :],
                                                   start=(q == 0), stop=(q == 3))
                        ins.then_inc(g_prod, 1)
                        if layer == 2:
                            pe.wait_ge(g_unit, t + 1)
                            for k in range(KT):
                                ins = nc.tensor.transpose(agg[0][:, k * NP:(k + 1) * NP],
                                                          g_mean[:, k * 128:(k + 1) * 128], ident[0:NP, 0:NP])
                            ins.then_inc(g_turned, 1)
                            pe.wait_ge(g_kept, t * 2 + (2 * NT + 2))
                            for k in range(KT):
                                ins = nc.tensor.matmul(own[1][0:NP, 0:D], g_t[:, k, :], w1[:, k, :],
                                                       start=(k == 0), stop=(k == 1))
                            ins.then_inc(g_prod, 1)
            if_general(pe, general_path)

        @block.scalar
        def _(act):
            act.dma_start(rows_a, dst[0:E].rearrange("(p n) -> p n", n=ROWS)).then_inc(rows_in, 16)
            act.dma_start(rows_b, dst[1:E + 1].rearrange("(p n) -> p n", n=ROWS)).then_inc(rows_in, 16)
            def hi_of(layer, j, b):
                nc.scalar.activation(messages[:, G5 * j + b, 0:D], msg[b % 4][0:NP, 0:D], ACT.Copy).then_inc(hi_ok, 1)

            def first_row(j):
                def hi(j, b):
                    j, b = (j - 1, b + G5) if b < 0 else (j, b)
                    act.wait_ge(msg_ok, G5 * j + b + 1)
                    hi_of(0, j, b)

                for b in range(G5):
                    tile = G5 * j + b
                    act.wait_ge(feat_read, tile + 1)
                    after(act, x_turned_stored[b], 16 * j)
                    after(act, msg_ok, tile - G5 + 1)
                    nc.scalar.activation(x_turned[:, b, :], turn[b % 2][:, 0:KT * NP],
                                         ACT.Copy).then_inc(xt_kept, 1)
                    if not (isinstance(j, int) and b == 0):
                        hi(j, b - 1)
                    act.wait_ge(xt_kept, tile + 1)
                    act.dma_start(feat_t[0, tile], x_turned[:, b, :]).then_inc(x_turned_stored[b], 16)
                return hi
            hi = first_row(0)
            with act.Fori(1, G5) as j:
                first_row(j)
            hi(G5, -1)
            act.wait_ge(keys_turned, 1)
            for bank, keys in ((own, key_src), (turn, key_dst)):
                nc.scalar.activation(keys[:, 0:4 * NP].rearrange("p (t g) -> p t g", t=4),
                                     bank[0][:, :].rearrange("p (t g) -> p t g", g=WIN)[:, :, 0:NP],
                                     ACT.Copy).then_inc(keys_kept, 1)
                nc.scalar.activation(keys[:, 4 * NP:NG], bank[1][:, 0:NP], ACT.Copy).then_inc(keys_kept, 1)
            act.wait_ge(bias_in, 16)
            act.wait_ge(win_w_in, 16)
            act.wait_ge(lo_ok, NT)
            for b in range(G5):
                act.wait_ge(x_turned_stored[b], 16 * G5)

            def keep_counts(j, b, units):
                for u in units:
                    m = BANKS[u]
                    act.wait_ge(summed, NB_ROW * j + b * NB_TILE + u + 1)
                    nc.scalar.activation(counts[:, :, bass.ds(j * NP + b * GT + BANK_STARTS[u], m)],
                                         built[u % 2][0:NP, 0:m * NP].rearrange(
                                             "p (m k) -> p k m", m=m), ACT.Copy).then_inc(kept, 1)
            for b in range(G5):
                keep_counts(0, b, range(NB_TILE))

            def keep_h(layer, j, b):
                j, b = (j - 1, b + G5) if b < 0 else (j, b)
                q, t = b % SLOTS, NT * layer + G5 * j + b
                act.wait_ge(h_turned, t + 1)
                after(act, feat_stored[q], 16 * (nth(layer, j, b) - 1))
                for k in range(KT):
                    ins = nc.scalar.activation(out_slot(q)[:, k, :], turn[0][:, k * NP:(k + 1) * NP], ACT.Relu,
                                               bias=bias_t[:, layer, k:k + 1])
                ins.then_inc(ht_kept, 1)
                act.wait_ge(ht_kept, t + 1)
                act.dma_start(feat_t[layer + 1, G5 * j + b], feat_out[:, q, 0:KT * NP]
                              ).then_inc(feat_stored[q], 16)

            def keep_both(j):
                for b in range(G5):
                    if not (isinstance(j, int) and b == 0):
                        keep_counts(j + 1, b, range(EARLY_BANKS))
                        keep_h(0, j, b - 1)
                        keep_counts(j + 1, b, range(EARLY_BANKS, NB_TILE))
                    else:
                        keep_counts(j + 1, b, range(NB_TILE))
            keep_both(0)
            with act.Fori(1, G5 - 1) as j:
                keep_both(j)
            for b in range(G5):
                keep_h(0, G5 - 1, b - 1)

            def keep_hi(layer):
                act.wait_ge(agg_ok, NT * layer)
                act.wait_ge(range_seen, 2 * NT * layer + 2)

                def row(j):
                    for b in range(G5):
                        act.wait_ge(feat_read, 2 * NT * layer + G5 * j + b + 1)
                        hi_of(layer, j, b)
                        if isinstance(j, int) and b == 1:
                            keep_h(layer - 1, G5, -1)
                rows(act, row)

            keep_hi(1)

            def keep_row(j):
                for b in range(G5):
                    if not (isinstance(j, int) and j == 0 and b == 0):
                        keep_h(1, j, b - 1)
            keep_row(0)
            with act.Fori(1, 3) as j:
                keep_row(j)
            act.wait_ge(edges_turned, 1)
            nc.scalar.activation(turned, turn[1][:, 0:3 * GW].rearrange("p (q g) -> p q g", q=3),
                                 ACT.Copy).then_inc(act_step, 1)
            keep_row(3)
            keep_row(4)
            act.wait_ge(scattered, GW)
            for k, bank in enumerate((mix, turn[1])):
                nc.scalar.activation(w1[:, k, :], bank[:, 0:D], ACT.Copy).then_inc(w1_ok, 1)
            keep_hi(2)

            def finish_ut(j, b):
                j, b = (j - 1, b + G5) if b < 0 else (j, b)
                t = G5 * j + b
                act.wait_ge(h_turned, 2 * NT + t + 1)
                after(act, mixed, G5 * j + before(b, G5, 2) + 1)
                nc.scalar.activation(ut_sb[:, b % 2, :, :],
                                     turn[0][:, 0:KT * NP].rearrange("p (k n) -> p k n", k=KT),
                                     ACT.Copy).then_inc(ht_kept, 1)
                act.wait_ge(var2_ok, t + 1)
                nc.scalar.activation(small[:, 20:21], small[:, 19:20], ACT.Sqrt, bias=small[:, 40:41]
                                     ).then_inc(root2_ok, 1)

            def row(j):
                for b in range(G5):
                    if not (isinstance(j, int) and b == 0):
                        finish_ut(j, b - 1)
                    act.wait_ge(var_ok, G5 * j + b + 1)
                    nc.scalar.activation(small[:, 8:9], small[:, 7:8], ACT.Sqrt, bias=small[:, 40:41]
                                         ).then_inc(root_ok, 1)
            rows(act, row)
            finish_ut(G5, -1)

            def general_path():
                act.dma_start(g_bias, bias.rearrange("(a l) d -> a (l d)", a=1).broadcast_to([NP, LAYERS * D])
                              ).then_inc(g_in, 16)
                act.wait_ge(g_zeroed, 1)
                for half in range(2):
                    act.dma_start(g_matrix.rearrange("(p n) a -> p (n a)", n=1024)[:, half * 512:half * 512 + 512],
                                  g_zero[0:64, :]).then_inc(g_cleared, 16)
                act.wait_ge(g_cleared, 32)
                with act.Fori(0, ROWS) as r:
                    act.dma_start(g_pair, pairs[bass.ds(r * NP, NP), :]).then_inc(g_pair_in, 16)
                    act.dma_start(g_w, ew[bass.ds(r * NP, NP)].rearrange("(p a) -> p a", a=1)).then_inc(g_w_in, 16)
                    act.wait_ge(g_scat, r * 16 + 16)
                act.dma_start(w1, g_matrix.rearrange("(k p n) a -> p k (n a)", k=KT, p=128)).then_inc(g_in, 16)
                for layer in range(LAYERS):
                    with act.Fori(0, ROWS) as r:
                        act.dma_start(g_pair, pairs[bass.ds(r * NP, NP), :]).then_inc(g_pair_in, 16)
                        act.wait_ge(g_added, (r + (layer * ROWS + 1)) * NT)
                    act.dma_start(wn[:, :, :], neigh_w[layer]).then_inc(g_in, 16)
                    act.dma_start(ws[:, :, :], self_w[layer]).then_inc(g_in, 16)
                    feat = x if layer == 0 else g_feat[layer - 1]
                    to = out if layer == LAYERS - 1 else g_feat[layer]
                    with act.Fori(0, NT) as t:
                        act.dma_start(g_h, feat[bass.ds(t * NP, NP), :]).then_inc(g_tile_in, 16)
                        act.dma_start(g_x, x[bass.ds(t * NP, NP), :]).then_inc(g_tile_in, 16)
                        for q in range(2 if layer == 2 else 1):
                            act.wait_ge(g_turned, t + (NT * layer + 1) if layer < 2 else t * 2 + (2 * NT + 1 + q))
                            n = 4 if q == 0 else 2
                            nc.scalar.activation(g_t[:, 0:n, :],
                                                 agg[0][:, 0:n * NP].rearrange("p (q n) -> p q n", q=n),
                                                 ACT.Copy).then_inc(g_kept, 1)
                            if layer == 2:
                                act.wait_ge(g_var, t * 2 + (1 + q))
                                nc.scalar.activation(g_c[:, 8:9], g_c[:, 7:8], ACT.Sqrt, bias=small[:, 40:41]
                                                     ).then_inc(g_root, 1)
                        act.wait_ge(g_st_ok, t + (NT * layer + 1))
                        act.dma_start(to[bass.ds(t * NP, NP), :], g_st).then_inc(g_stored, 16)
                        act.wait_ge(g_stored, t * 16 + 16 * (NT * layer + 1))
                act.wait_ge(g_stored, 16 * NT * LAYERS)
            if_general(act, general_path)

        @block.vector
        def _(dve):
            step = Steps(dve, dve_step)
            v = nc.vector
            dve.wait_ge(constants, 3)
            step(v.tensor_copy(thr, thr_i))
            step(v.memset(small[:, 40:41], EPS))
            dve.wait_ge(heads_in, 16)
            step(v.tensor_copy(heads_f, heads_i))
            for t in range(5):
                step(v.tensor_scalar(junk, heads_f, thr[:, t:t + 1], 0.0, ALU.is_lt, ALU.add,
                                     accum_out=cnt[:, t:t + 1]))
            step(v.tensor_scalar(head_row, cnt, 1.0, 0.0, ALU.subtract, ALU.max))
            v.tensor_copy(row_i, head_row).then_inc(rows_at, 1)
            dve.wait_ge(rows_in, 32)
            step(v.tensor_tensor(junk, rows_a, rows_b, ALU.is_gt))
            step(v.tensor_reduce(small[:, 41:42], junk, AX.X, ALU.max))

            def first_rest(j, b):
                tile = G5 * j + b
                dve.wait_ge(hi_ok, tile + 1)
                v.tensor_tensor(rest_all[:, tile, :], msg[b % 4][0:NP, 0:D], messages[:, tile, 0:D],
                                ALU.subtract).then_inc(rest_ok, 1)

            def first_rests(j):
                for b in range(G5):
                    first_rest(j, b)
            first_rests(0)
            dve.wait_ge(found_in, 80)
            step(v.tensor_copy(found_f, found_i))
            for t in range(5):
                step(v.tensor_scalar(junk[:, 0:NP], found_f[:, t, :], thr[:, t:t + 1], 0.0, ALU.is_lt, ALU.add,
                                     accum_out=fine[:, t:t + 1]))
            step(v.scalar_tensor_tensor(out=head_row, in0=head_row, scalar=float(NP), in1=fine,
                                        op0=ALU.mult, op1=ALU.add))
            v.tensor_copy(start_i, head_row).then_inc(windows_at, 1)
            def split(layer, tile, b):
                dve.wait_ge(hi_ok, NT * layer + tile + 1)
                after(dve, lo_ok, NT * layer + tile - b + before(b, G5, 2) + 1)
                v.tensor_tensor(rest[:, b % 2, :], msg[b % 4][0:NP, 0:D], messages[:, tile, 0:D],
                                ALU.subtract).then_inc(rest_ok, 1)
                dve.wait_ge(rest_ok, NT * layer + tile + 1)
                v.tensor_scalar(messages[:, tile, D:2 * D], rest[:, b % 2, :], LO, None, ALU.mult).then_inc(lo_ok, 1)

            def split_rows(layer):
                dve.wait_ge(agg_ok, NT * layer)
                dve.wait_ge(h_ok, NT * layer)

                def row(j):
                    for b in range(G5):
                        split(layer, G5 * j + b, b)
                rows(dve, row)
            with dve.Fori(1, G5 - 1) as j:
                first_rests(j)
            dve.wait_ge(win_in, 80)
            step(v.tensor_copy(f_src, win[:, :, :, 1]))
            step(v.tensor_copy(f_dst, win[:, :, :, 0]))
            for t in range(5):
                step(v.tensor_scalar(jd[:, t, :], f_dst[:, t, :], thr[:, t:t + 1], None, ALU.subtract))
            step(v.tensor_scalar(va, jd, 0.0, None, ALU.is_ge))
            step(v.scalar_tensor_tensor(out=va, in0=jd, scalar=4.0, in1=va, op0=ALU.is_le, op1=ALU.mult))
            first_rest(G5 - 1, 0)
            step(v.tensor_scalar(vb, f_src, 1.0 / NG, -0.4992, ALU.mult, ALU.add))
            step(v.tensor_scalar(vb, vb, MAGIC, None, ALU.add))
            step(v.tensor_scalar(vb, vb, MAGIC, None, ALU.subtract))
            step(v.scalar_tensor_tensor(out=src, in0=vb, scalar=-float(NG), in1=f_src, op0=ALU.mult, op1=ALU.add))
            first_rest(G5 - 1, 1)
            step(v.tensor_scalar(vc, src, 1.0 / G5, -0.4, ALU.mult, ALU.add))
            step(v.tensor_scalar(vc, vc, MAGIC, None, ALU.add))
            step(v.tensor_scalar(vc, vc, MAGIC, None, ALU.subtract))
            step(v.scalar_tensor_tensor(out=vd, in0=vc, scalar=-float(G5), in1=src, op0=ALU.mult, op1=ALU.add))
            for b in range(2, G5):
                first_rest(G5 - 1, b)
            step(v.scalar_tensor_tensor(out=vd, in0=vd, scalar=5.0, in1=jd, op0=ALU.mult, op1=ALU.add))
            step(v.scalar_tensor_tensor(out=vd, in0=vb, scalar=25.0, in1=vd, op0=ALU.mult, op1=ALU.add))
            step(v.scalar_tensor_tensor(out=vd, in0=vd, scalar=1.0, in1=va, op0=ALU.add, op1=ALU.mult))
            v.tensor_scalar(vd, vd, 1.0, None, ALU.subtract).then_inc(keys_ok, 1)
            step(v.scalar_tensor_tensor(out=slot_j, in0=jd, scalar=1.0, in1=va, op0=ALU.add, op1=ALU.mult))
            step(v.tensor_copy(win_s[:, :], f_src[:, 0, :]))
            step(v.tensor_scalar(win_j[:, :], slot_j[:, 0, :], 1.0, None, ALU.subtract))
            dve.wait_ge(keys_kept, 4)

            def degree_of(t, j):
                step(v.tensor_scalar(no_use, slot_j[:, t, :], float(j + 1), 0.0, ALU.is_equal, ALU.add,
                                     accum_out=degree[:, G5 * t + j:G5 * t + j + 1]))

            def make_hot(j, b, degrees=False):
                for c, n in enumerate(CHUNKS):
                    w = b * len(CHUNKS) + c
                    after(dve, summed, NB_ROW * j + 2 * (w - 2) + 2)
                    for q, keys in enumerate((key_src, key_dst)):
                        ins = v.tensor_tensor(
                            hot[:, w % 2, q, 0:NP * n].rearrange("p (v n) -> p v n", n=n), ramp[:, :, 0:n],
                            keys[:, bass.ds(j * NP + b * GT + STARTS[c], n)].unsqueeze(1).broadcast_to([128, NP, n]),
                            ALU.is_equal)
                    ins.then_inc(hot_ok, 1)
                    if degrees:
                        for i in range(c, G5, len(CHUNKS)):
                            degree_of(b, i)
            for b in range(G5):
                make_hot(0, b, degrees=True)
            step(v.tensor_scalar(inv_deg[:, :], degree[:, :], 1.0, None, ALU.max))
            step(v.reciprocal(inv_deg[:, :], inv_deg[:, :]))
            step(v.scalar_tensor_tensor(out=inv_deg[:, :], in0=degree[:, :], scalar=0.0, in1=inv_deg[:, :],
                                        op0=ALU.is_gt, op1=ALU.mult))
            step.done()

            def make_h(layer, j, b):
                t = NT * layer + G5 * j + b
                dve.wait_ge(agg_ok, t + 1)
                step(v.tensor_scalar(agg_sb[:, b % 2, :], agg[b % 3][0:NP, D:2 * D], 1.0 / LO, None, ALU.mult))
                step(v.tensor_tensor(agg_sb[:, b % 2, :], agg_sb[:, b % 2, :], agg[b % 3][0:NP, 0:D], ALU.add))
                after(dve, h_turned, NT * layer + G5 * j + before(b, G5, 2) + 1)
                return v.scalar_tensor_tensor(out=h_sb[:, b % 2, :], in0=agg_sb[:, b % 2, :],
                                              scalar=inv_deg[:, bass.ds(G5 * j + b, 1)], in1=own[b % 2][0:NP, 0:D],
                                              op0=ALU.mult, op1=ALU.add)

            def row0(j):
                step.row(j, 2 * G5)
                for b in range(G5):
                    make_hot(j + 1, b)
                    make_h(0, j, b).then_inc(h_ok, 1)
            row0(0)
            with dve.Fori(1, G5 - 1) as j:
                row0(j)
            step.row(G5 - 1, 2 * G5)
            for b in range(G5):
                make_h(0, G5 - 1, b).then_inc(h_ok, 1)
            step.end_rows(2 * G5)
            dve.wait_ge(summed, NB_ROW * G5)
            dve.wait_ge(late_ok, 2)
            step(v.memset(win_k, 0.0))
            step(v.tensor_scalar(win_v, win_j[0:GW, :], 0.0, None, ALU.is_ge))
            step(v.scalar_tensor_tensor(out=win_v, in0=win_s[0:GW, :], scalar=float(D), in1=win_v,
                                        op0=ALU.is_lt, op1=ALU.mult))
            step(v.scalar_tensor_tensor(out=win_q, in0=win_s[0:GW, :], scalar=5.0, in1=win_j[0:GW, :],
                                        op0=ALU.mult, op1=ALU.add))
            step(v.scalar_tensor_tensor(out=win_k[:, 0:WIN], in0=win_q, scalar=1.0, in1=win_v,
                                        op0=ALU.add, op1=ALU.mult))
            step.done()
            split_rows(1)

            def last_use(i):
                mine = win_k[:, bass.ds(i, NL)].unsqueeze(2).broadcast_to([GW, NL, WIN])
                theirs = win_k[:, 0:WIN].unsqueeze(1).broadcast_to([GW, NL, WIN])
                step(v.tensor_tensor(same, mine, theirs, ALU.is_equal))
                step(v.tensor_tensor(same, same, slot_no.unsqueeze(1).broadcast_to([GW, NL, WIN]), ALU.mult))
                step(v.tensor_reduce(last[:, bass.ds(i, NL)], same, AX.X, ALU.max))

            def make_factor(g):
                after(dve, scattered, g - 1)
                v.tensor_scalar(factor[:, g % 2, :], ramp_d, turned[:, 1, g:g + 1], turned[:, 0, g:g + 1],
                                ALU.is_equal, ALU.mult).then_inc(factor_ok, 1)

            def row1(j):
                step.row(j, 5 * G5)
                for b in range(G5):
                    last_use((G5 * j + b) * NL)
                    make_h(1, j, b).then_inc(h_ok, 1)
            row1(0)
            with dve.Fori(1, 3) as j:
                row1(j)
            step.base += 3 * 5 * G5
            step.start, step.k = step.base, 0
            step(v.tensor_tensor(last[:, 0:WIN], last[:, 0:WIN], slot_no, ALU.is_equal))
            step(v.scalar_tensor_tensor(out=last[:, 0:WIN], in0=win_k[:, 0:WIN], scalar=0.5, in1=last[:, 0:WIN],
                                        op0=ALU.is_gt, op1=ALU.mult))
            dve.wait_ge(win_w_in, 16)
            v.tensor_tensor(win_w[0:GW, :], win_w[0:GW, :], last[:, 0:WIN], ALU.mult).then_inc(edges_ok, 1)
            for t in range(3 * G5, NT):
                if t == 3 * G5 + 1:
                    dve.wait_ge(act_step, 1)
                    for j in range(5):
                        ins = v.tensor_scalar(hot_j[:, :, j], turned[:, 2, :], float(j), None, ALU.is_equal)
                    step(ins)
                first = (t - 3 * G5 - 1) * GS
                if 0 <= first < GW:
                    for g in range(first, first + GS):
                        make_factor(g)
                make_h(1, t // G5, t % G5).then_inc(h_ok, 1)
            step.done()
            split_rows(2)
            def norm(value, at, t, var, root):
                step(v.bn_stats(small[:, at:at + 6], value))
                v.memset(small[:, 60:61], 0.0)
                v.bn_aggr(small[:, at + 6:at + 8], small[:, at:at + 6]).then_inc(var, 1)
                dve.wait_ge(root, t + 1)
                step(v.reciprocal(small[:, at + 9:at + 10], small[:, at + 8:at + 9]))

            def nth2(j, b):
                return (3, 2)[b % 2] * j + b // 2 + 1

            def finish(j, b):
                j, b = (j - 1, b + G5) if b < 0 else (j, b)
                t = G5 * j + b
                r = res_sb[:, b % 2, :]
                dve.wait_ge(mixed, t + 1)
                after(dve, out_stored[b % 2], 16 * (nth2(j, b) - 1))
                v.tensor_tensor(r, h_sb[:, b % 2, :], mix[0:NP, 0:D], ALU.add).then_inc(out_ok, 1)
                dve.wait_ge(out_ok, t + 1)
                norm(r, 12, t, var2_ok, root2_ok)
                v.tensor_scalar(r, r, small[:, 18:19], small[:, 21:22], ALU.subtract, ALU.mult).then_inc(res_ok, 1)

            def row2(j):
                step.row(j, 7 * G5)
                if not isinstance(j, int):
                    step.start = step.start - 2
                for b in range(G5):
                    if not (isinstance(j, int) and b == 0):
                        finish(j, b - 1)
                    t = G5 * j + b
                    make_h(2, j, b).then_inc(own_read, 1)
                    dve.wait_ge(own_read, t + 1)
                    z = h_sb[:, b % 2, :]
                    dve.wait_ge(xb_ok, t + 1)
                    step(v.tensor_tensor(z, z, feat_out[0:NP, b % SLOTS, :], ALU.add))
                    norm(z, 0, t, var_ok, root_ok)
                    v.tensor_scalar(z, z, small[:, 6:7], small[:, 9:10], ALU.subtract, ALU.mult).then_inc(h_ok, 1)
            row2(0)
            with dve.Fori(1, G5) as j:
                row2(j)
            step.base, step.k = step.base + 5 * 7 * G5 - 2, 0
            step.start = step.base
            dve.wait_ge(range_seen, 2 * NT * LAYERS + 2)
            step(v.tensor_reduce(small[:, 42:43], squares[:, :], AX.X, ALU.add))
            step(v.tensor_scalar(small[:, 42:43], small[:, 42:43], HI_MAX * HI_MAX, None, ALU.is_lt))
            step(v.scalar_tensor_tensor(out=small[:, 43:44], in0=small[:, 41:42], scalar=1.0,
                                        in1=small[:, 42:43], op0=ALU.add, op1=ALU.subtract))
            step(v.tensor_reduce(small[:, 44:45], degree[:, :], AX.X, ALU.add))
            v.memset(small[:, 45:46], 1.0).then_inc(checks_ok, 1)
            dve.wait_ge(checked, 1)
            step(v.tensor_scalar(small[0:1, 46:47], turn[1][0:1, 1:2], float(E), None, ALU.not_equal))
            step(v.tensor_scalar(small[0:1, 47:48], turn[1][0:1, 0:1], 0.0, None, ALU.is_gt))
            step(v.tensor_tensor(small[0:1, 46:47], small[0:1, 46:47], small[0:1, 47:48], ALU.max))
            v.tensor_copy(general[0:1, 0:1], small[0:1, 46:47]).then_inc(general_ok, 1)
            finish(G5, -1)

            def general_path():
                dve.wait_ge(g_const, 3)
                one = Steps(dve, g_step)
                one(v.tensor_copy(g_c[:, 0:1], g_part))
                one(v.tensor_scalar(g_later, g_ramp[:, 0:NP], g_c[:, 0:1], None, ALU.is_gt))
                one.done()
                per = 7
                with dve.Fori(0, ROWS) as r:
                    one.row(r, per)
                    dve.wait_ge(g_pair_in, r * 16 + 16)
                    one(v.tensor_copy(g_c[:, 1:3], g_pair))
                    one(v.tensor_scalar(g_c[:, 3:5], g_c[:, 1:3], float(D), None, ALU.is_lt))
                    one(v.tensor_tensor(g_c[:, 3:4], g_c[:, 3:4], g_c[:, 4:5], ALU.mult))
                    one(v.scalar_tensor_tensor(out=g_c[:, 5:6], in0=g_c[:, 2:3], scalar=float(D), in1=g_c[:, 1:2],
                                               op0=ALU.mult, op1=ALU.add))
                    one(v.scalar_tensor_tensor(out=g_c[:, 5:6], in0=g_c[:, 5:6], scalar=-float(D * D),
                                               in1=g_c[:, 3:4], op0=ALU.add, op1=ALU.mult))
                    v.tensor_scalar(g_keys, g_zero[:, 0:NP], g_c[:, 5:6], None, ALU.add).then_inc(g_key_ok, 1)
                    dve.wait_ge(g_keys_t, r + 1)
                    one(v.scalar_tensor_tensor(out=g_same, in0=turn[0][0:NP, 0:NP], scalar=g_c[:, 5:6], in1=g_later,
                                               op0=ALU.is_equal, op1=ALU.mult))
                    one(v.tensor_reduce(g_c[:, 6:7], g_same, AX.X, ALU.max))
                    v.scalar_tensor_tensor(out=g_c[:, 10:11], in0=g_c[:, 6:7], scalar=float(D * D), in1=g_c[:, 5:6],
                                           op0=ALU.mult, op1=ALU.add).then_inc(g_step2, 1)
                    dve.wait_ge(g_step2, r + 1)
                    v.tensor_scalar(g_idx, g_c[:, 10:11], float(D * D), None, ALU.add).then_inc(g_idx_ok, 1)
                assert one.k == per
                one.base += ROWS * per
                one.start, one.k = one.base, 0
                dve.wait_ge(g_in, 32)

                def general_norm(value, t, q):
                    one(v.bn_stats(g_c[:, 12:18], value))
                    v.memset(g_c[:, 30:31], 0.0)
                    v.bn_aggr(g_c[:, 6:8], g_c[:, 12:18]).then_inc(g_var, 1)
                    dve.wait_ge(g_root, t * 2 + (1 + q))
                    one(v.reciprocal(g_c[:, 9:10], g_c[:, 8:9]))

                for layer in range(LAYERS):
                    one(v.memset(g_sum, 0.0))
                    one.done()
                    with dve.Fori(0, ROWS) as r:
                        one.row(r, 1)
                        dve.wait_ge(g_pair_in, r * 16 + 16 * ((layer + 1) * ROWS + 1))
                        v.tensor_copy(g_idx, g_pair[:, 1:2]).then_inc(g_got, 1)
                        one(v.tensor_copy(g_c[:, 1:2], g_pair[:, 0:1]))
                        v.tensor_scalar(g_hot, g_ramp, g_c[:, 1:2], None, ALU.is_equal).then_inc(g_hot_ok, 1)
                        banks = agg + own + turn + [mix]
                        for t in range(NT):
                            dve.wait_ge(g_summed, r * NT + (layer * ROWS * NT + t + 1))
                            v.tensor_tensor(g_sum[:, t, :], g_sum[:, t, :], banks[t % len(banks)][0:NP, 0:D + 1],
                                            ALU.add).then_inc(g_added, 1)
                    one.base += ROWS
                    one.start, one.k = one.base, 0
                    dve.wait_ge(g_added, (layer + 1) * ROWS * NT)
                    per = 3 if layer < 2 else 9
                    with dve.Fori(0, NT) as t:
                        one.row(t, per)
                        at = t + (NT * layer + 1)
                        degrees = g_sum[:, t, D:D + 1]
                        one(v.tensor_scalar(g_c[:, 2:3], degrees, 1.0, None, ALU.max))
                        one(v.reciprocal(g_c[:, 3:4], g_c[:, 2:3]))
                        v.tensor_scalar(g_mean, g_sum[:, t, 0:D], g_c[:, 3:4], None, ALU.mult).then_inc(g_mean_ok, 1)
                        dve.wait_ge(g_prod, at if layer < 2 else t * 2 + (2 * NT + 1))
                        one(v.tensor_tensor(g_st, own[0][0:NP, 0:D], g_bias[:, layer * D:(layer + 1) * D], ALU.add))
                        if layer < 2:
                            v.tensor_scalar(g_st, g_st, 0.0, None, ALU.max).then_inc(g_st_ok, 1)
                        else:
                            dve.wait_ge(g_tile_in, at * 32)
                            one(v.tensor_tensor(g_st, g_st, g_x, ALU.add))
                            general_norm(g_st, t, 0)
                            v.tensor_scalar(g_mean, g_st, g_c[:, 6:7], g_c[:, 9:10], ALU.subtract, ALU.mult
                                            ).then_inc(g_unit, 1)
                            dve.wait_ge(g_prod, t * 2 + (2 * NT + 2))
                            one(v.tensor_tensor(g_st, g_mean, own[1][0:NP, 0:D], ALU.add))
                            general_norm(g_st, t, 1)
                            v.tensor_scalar(g_st, g_st, g_c[:, 6:7], g_c[:, 9:10], ALU.subtract, ALU.mult
                                            ).then_inc(g_st_ok, 1)
                    assert one.k == per, (one.k, per)
                    one.base += NT * per
                    one.start, one.k = one.base, 0
            if_general(dve, general_path)


_OUT = (N, D)


def kernel(x, src, dst, edge_weight, L0_gnn_W_self, L0_gnn_W_neigh, L0_gnn_bias):
    import numpy as np
    import concourse.bacc as bacc
    from concourse.bass_utils import run_bass_kernel_spmd as run

    src, dst, ew = np.asarray(src), np.asarray(dst), np.asarray(edge_weight)
    dst_pad = np.concatenate([dst, np.full(WIN, N, dst.dtype)])
    src_pad = np.concatenate([src, np.zeros(WIN, src.dtype)])
    arrays = {
        "x": np.asarray(x),
        "pairs": np.ascontiguousarray(np.stack([dst_pad, src_pad], 1)),
        "dst": dst_pad,
        "heads": np.ascontiguousarray(dst[::NP]),
        "ew": np.concatenate([ew, np.zeros(WIN, ew.dtype)]),
        "w_self": np.asarray(L0_gnn_W_self),
        "w_neigh": np.asarray(L0_gnn_W_neigh),
        "bias": np.asarray(L0_gnn_bias),
        "bias_cols": np.ascontiguousarray(np.asarray(L0_gnn_bias).reshape(LAYERS, KT, 128).transpose(2, 0, 1)),
    }
    nc = bacc.Bacc("TRN2", target_bir_lowering=False, num_devices=1)
    args = [nc.dram_tensor(k, v.shape, mybir.dt.from_np(v.dtype), kind="ExternalInput").ap()
            for k, v in arrays.items()]
    out = nc.dram_tensor("out", _OUT, F32, kind="ExternalOutput").ap()
    feat_t = nc.dram_tensor("feat_t", (LAYERS, NT, 128, KT * NP), F32, kind="Internal").ap()
    g_feat = [nc.dram_tensor(f"g_feat{q}", (N, D), F32, kind="Internal").ap() for q in range(LAYERS - 1)]
    g_matrix = nc.dram_tensor("g_matrix", (D * D, 1), F32, kind="Internal").ap()
    build(nc, *args, out, feat_t, g_feat, g_matrix)
    return run(nc, [arrays], core_ids=[0]).results[0]["out"]
```

```python
from contextlib import ExitStack

import concourse.bass as bass
from concourse import mybir

ALU = mybir.AluOpType
ACT = mybir.ActivationFunctionType
AX = mybir.AxisListType
F32 = mybir.dt.float32
F16 = mybir.dt.float16
BF16 = mybir.dt.bfloat16
I32 = mybir.dt.int32

N = 3125
D = 256
E = 53125
LAYERS = 3
NP = 125
NT = N // NP
G5 = 5
NG = N // G5
GT = NG // NT
WIN = 128
ROWS = E // NP
KT = D // 128
LO = 2048.0
CHUNKS = (7, 6, 6, 6)
CW = max(CHUNKS)
STARTS = [sum(CHUNKS[:c]) for c in range(len(CHUNKS))]
BANKS = (4, 3, 3, 3, 3, 3, 3, 3)
BANK_STARTS = [sum(BANKS[:u]) for u in range(len(BANKS))]
NB_TILE = len(BANKS)
NB_ROW = G5 * NB_TILE
NC_ROW = G5 * len(CHUNKS)
BUILD_SUMS = 24
EARLY_BANKS = 4
GW = 56
GH = GW // 2
GS = 7
SCATTER_FROM = NT - GW // GS
NL = 9
LW = 15 * NL
EPS = 1e-5
MAGIC = 12582912.0
HI_MAX = 60000.0
SLOTS = 3
WINDOWS_AT = 10


def before(v, period, slots):
    if v >= slots:
        return v - slots
    last = (period - 1) - ((period - 1 - v) % slots)
    return last - period


def after(engine, sem, count):
    if isinstance(count, int) and count <= 0:
        return
    engine.wait_ge(sem, count)


class Steps:

    def __init__(self, engine, sem):
        self.engine, self.sem, self.base, self.start, self.k = engine, sem, 0, 0, 0

    def row(self, j, per):
        self.start, self.k = self.base + per * j, 0

    def end_rows(self, per):
        assert self.k == per, (self.k, per)
        self.base += G5 * per
        self.start, self.k = self.base, 0

    def __call__(self, instruction):
        instruction.then_inc(self.sem, 1)
        self.k += 1
        self.engine.wait_ge(self.sem, self.start + self.k)

    def done(self):
        self.base += self.k
        self.start, self.k = self.base, 0


def build(nc, x, pairs, dst, heads, ew, w_self, w_neigh, bias, bias_cols, out, feat_t, g_feat, g_matrix):
    with ExitStack() as ctx:
        def sb(name, shape, dt):
            return ctx.enter_context(nc.sbuf_tensor(name, shape, dt))

        def ps(name, shape):
            return ctx.enter_context(nc.psum_tensor(name, shape, F32))

        def sem(name):
            return ctx.enter_context(nc.semaphore(name))

        counts_mem_wide = sb("counts", [128, NT * G5 * NG + 1], F16)
        counts_mem = counts_mem_wide[0:NP, :]
        counts = counts_mem[:, 0:NT * G5 * NG].rearrange("p (a g) -> p a g", g=NG)
        messages = sb("messages", [NP, NT, 2 * D], F16)
        hot_mem = sb("hot", [128, 4 * NP * CW], F16)
        hot = hot_mem[:, :].rearrange("p (r s n) -> p r s n", r=2, s=2)
        early = sb("early", [128, 2 * 1088], F16)
        feat_in = sb("feat_in", [128, SLOTS, D], F32)
        feat_out = sb("feat_out", [128, SLOTS, D], F32)
        wn = sb("wn", [128, KT, D], F32)
        ws = sb("ws", [128, KT, D], F32)
        ident = sb("ident", [128, 128], F32)
        bias_t = sb("bias_t", [128, LAYERS, KT], F32)
        win_w = sb("win_w", [NP, WIN], F32)
        win_s = sb("win_s", [NP, WIN], F32)
        win_j = sb("win_j", [NP, WIN], F32)
        rest_t = sb("rest", [128, 2 * D], F32)
        h_sb = sb("h", [NP, 2, D], F32)
        rest = rest_t[0:NP, :].rearrange("p (r f) -> p r f", r=2)
        degree = sb("degree", [NP, NT], F32)
        inv_deg = sb("inv_deg", [NP, NT], F32)
        square = sb("square", [NP, D], F32)
        squares = sb("squares", [NP, D], F32)
        small = sb("small", [NP, 64], F32)
        general = sb("general", [1, 1], I32)

        ramp = early[:, 0:NP * CW].rearrange("p (v n) -> p v n", n=CW)
        key_src = early[:, NP * CW:NP * CW + NG]
        key_dst = early[:, NP * CW + NG:NP * CW + 2 * NG]
        h_16 = h_sb[:, :, :].rearrange("p r f -> p (r f)").bitcast(F16)
        slot_j, no_use = h_16[:, 0:G5 * WIN].rearrange("p (k n) -> p k n", k=G5), h_16[:, 768:768 + WIN]
        late = early[:, :].bitcast(F32)
        w1 = late[:, 0:KT * D].rearrange("p (k n) -> p k n", k=KT)
        bias_row = late[0:NP, KT * D:KT * D + D]
        ramp_d = late[:, 768:768 + D]
        slot_no = early[0:GW, 2048:2048 + WIN]

        tmp, tmp_i = counts_mem[:, :].bitcast(F32), counts_mem[:, :].bitcast(I32)

        def area(base, k, n, view=tmp):
            return view[:, base:base + k * n].rearrange("p (k n) -> p k n", k=k)
        rows_a, rows_b = tmp_i[:, 0:ROWS], tmp_i[:, 512:512 + ROWS]
        heads_i, heads_f = tmp_i[:, 1024:1024 + ROWS], tmp[:, 1536:1536 + ROWS]
        junk = tmp[:, 2048:2048 + ROWS]
        found_i, found_f = area(2560, 5, NP, tmp_i), area(3200, 5, NP)
        win_flat = area(4096, 5, 2 * WIN, tmp_i)
        win = win_flat.rearrange("p k (n two) -> p k n two", two=2)
        src, jd = area(5632, 5, WIN), area(6272, 5, WIN)
        va, vb, vc, vd = (area(7168 + 640 * q, 5, WIN) for q in range(4))
        f_src = area(10368, 5, WIN)
        thr_i, thr = tmp_i[:, 11008:11013], tmp[:, 11016:11021]
        cnt, fine, head_row = tmp[:, 11024:11029], tmp[:, 11032:11037], tmp[:, 11040:11045]
        row_i, start_i = tmp_i[:, 11048:11053], tmp_i[:, 11056:11061]
        x_turned = area(11072, G5, KT * NP, counts_mem_wide[:, :].bitcast(F32))
        rest_all = area(12352, NT, D)
        lo_scale = tmp[:, 18752:18752 + D]

        work = hot_mem[:, :].bitcast(F32)
        same = hot_mem[0:GW, 0:NL * WIN].rearrange("p (i n) -> p i n", n=WIN)
        win_k, last = hot_mem[0:GW, 1152:1152 + LW], hot_mem[0:GW, 1288:1288 + LW]
        win_v, win_q = work[0:GW, 712:712 + WIN], work[0:GW, 840:840 + WIN]
        factor = work[:, 712:712 + D].bitcast(BF16).rearrange("p (q f) -> p q f", q=2)
        turned = work[:, 968:968 + 3 * GW].rearrange("p (q g) -> p q g", q=3)
        hot_j = work[:, 1136:1136 + 5 * GW // 2].bitcast(BF16).rearrange("p (g j) -> p g j", j=5)
        parts = hot_mem[:, 2552:2552 + 15 * GW].bitcast(BF16).rearrange("p (q g j) -> p q g j", q=3, j=5)
        part = work[:, 1696:1696 + GW // 2].bitcast(BF16)
        rest_of = [rest[:, 0, :], rest[:, 1, :], work[0:NP, 1276:1276 + D]]
        ut_sb = work[:, 0:2 * D].rearrange("p (q k n) -> p q k n", q=2, k=KT)[:, :, :, 0:NP]
        res_sb = work[0:NP, 512:512 + 2 * D].rearrange("p (q f) -> p q f", q=2)

        agg = [ps(f"agg{q}", [128, 512]) for q in range(3)]
        own = [ps(f"own{q}", [128, 512]) for q in range(2)]
        turn = [ps(f"turn{q}", [128, 512]) for q in range(2)]
        mix = ps("mix", [128, 512])
        built = [turn[1], mix]
        msg = [own[1], agg[0], agg[2], own[0], agg[1]]

        rows_in, heads_in = sem("rows_in"), sem("heads_in")
        found_in, win_in, win_w_in = [sem(f"found_in{t}") for t in range(5)], sem("win_in"), sem("win_w_in")
        bias_in, bias_row_in, wn_in, ws_in = sem("bias_in"), sem("bias_row_in"), sem("wn_in"), sem("ws_in")
        feat_loaded = [sem(f"feat_loaded{q}") for q in range(G5)]
        x_turned_stored = [sem(f"x_turned_stored{q}") for q in range(G5)]
        feat_stored = [sem(f"feat_stored{q}") for q in range(SLOTS)]
        x_loaded = [sem(f"x_loaded{q}") for q in range(SLOTS)]
        out_stored = [sem(f"out_stored{q}") for q in range(2)]
        constants, pool_step = sem("constants"), sem("pool_step")
        rows_at, windows_at = sem("rows_at"), sem("windows_at")
        dve_step, keys_ok, keys_turned = sem("dve_step"), sem("keys_ok"), sem("keys_turned")
        edges_kept = sem("edges_kept")
        keys_kept = sem("keys_kept")
        hot_ok, summed, kept = sem("hot_ok"), sem("summed"), sem("kept")
        xt_kept, feat_read = sem("xt_kept"), sem("feat_read")
        msg_ok, hi_ok, rest_ok, lo_ok = sem("msg_ok"), sem("hi_ok"), sem("rest_ok"), sem("lo_ok")
        range_seen = sem("range_seen")
        agg_ok, h_ok = sem("agg_ok"), sem("h_ok")
        h_turned, ht_kept = sem("h_turned"), sem("ht_kept")
        late_ok, edges_ok, edges_turned, factor_ok, scattered, w1_ok = (
            sem("late_ok"), sem("edges_ok"), sem("edges_turned"), sem("factor_ok"), sem("scattered"), sem("w1_ok"))
        xb_ok, var_ok, root_ok, mixed, out_ok = (
            sem("xb_ok"), sem("var_ok"), sem("root_ok"), sem("mixed"), sem("out_ok"))
        checks_ok, checked, general_ok, special_done = (
            sem("checks_ok"), sem("checked"), sem("general_ok"), sem("special_done"))
        own_read = sem("own_read")
        var2_ok, root2_ok, res_ok = sem("var2_ok"), sem("root2_ok"), sem("res_ok")

        x_tiles = x.rearrange("(r p b) f -> r p b f", r=G5, p=NP)
        out_tiles = out.rearrange("(r p b) f -> r p b f", r=G5, p=NP)
        self_w = w_self.rearrange("l (k p) n -> l p k n", p=128)
        neigh_w = w_neigh.rearrange("l (k p) n -> l p k n", p=128)

        def wide_slot(q):
            return feat_in[:, q, :] if q < SLOTS else feat_out[:, (2, 0)[q - SLOTS], :]

        def h_of(layer, b):
            return rest[:, 1, :] if layer == 2 and b % G5 == 4 else h_sb[:, b % G5 % 2, :]

        def halves(slot):
            return slot[:, 0:KT * NP].rearrange("p (k n) -> p k n", k=KT)

        def out_slot(q):
            return feat_out[:, q, 0:KT * NP].rearrange("p (k n) -> p k n", k=KT)

        per_row = [len([b for b in range(G5) if b % SLOTS == q]) for q in range(SLOTS)]

        def nth(n, j, b):
            if b < 0:
                j, b = j - 1, b + G5
            return per_row[b % SLOTS] * (G5 * n + j) + b // SLOTS + 1

        def loaded(n, j, b):
            if n % 2:
                return per_row[b % SLOTS] * (G5 * (n // 2) + j) + b // SLOTS + 1 + G5 * ((n + 1) // 2)
            return (per_row[b] * G5 * (n // 2) if b < SLOTS else 0) + G5 * ((n + 1) // 2) + j + 1

        def rows(engine, body):
            body(0)
            with engine.Fori(1, G5) as j:
                body(j)

        def gen(base, n, view=tmp):
            return view[:, base:base + n]
        g_ramp, g_hot = gen(0, N), gen(3200, N)
        g_sum = area(6400, NT, D + 1)
        g_rows = gen(12900, D + 1)
        g_later, g_keys, g_same = gen(13200, NP), gen(13400, NP), gen(13600, NP)
        g_h, g_mean, g_x, g_st = gen(13800, D), gen(14100, D), gen(14400, D), gen(14700, D)
        g_bias = gen(15000, LAYERS * D)
        g_zero = gen(15800, 512)
        g_t = rest_t[:, 0:4 * NP].rearrange("p (q n) -> p q n", q=4)
        g_c = gen(16400, 32)
        g_pair, g_idx, g_part = gen(16500, 2, tmp_i), gen(16504, 1, tmp_i), gen(16506, 1, tmp_i)
        g_w = gen(16508, 1)
        g_hot_rows, g_step2 = sem("general_rows"), sem("general_place")
        g_carried = sem("general_carried")
        g_names = ("const", "step", "in", "pair", "got", "hot", "sum", "add", "key", "keys_t", "idx", "scat", "zeroed",
                   "tile", "mean", "tr", "kept", "prod", "var", "root", "unit", "st", "stored", "w", "cleared")
        (g_const, g_step, g_in, g_pair_in, g_got, g_hot_ok, g_summed, g_added, g_key_ok, g_keys_t, g_idx_ok, g_scat,
         g_zeroed, g_tile_in, g_mean_ok, g_turned, g_kept, g_prod, g_var, g_root, g_unit, g_st_ok, g_stored, g_w_in,
         g_cleared) = (sem("general_" + n) for n in g_names)

        def if_general(engine, body):
            engine.wait_ge(general_ok, 1)
            flag = engine.value_load(general[0:1, 0:1], min_val=0, max_val=1)
            with engine.If(flag > 0):
                engine.wait_ge(special_done, 1)
                body()

        block = ctx.enter_context(nc.Block())

        @block.sync
        def _(sp):
            sp.dma_start(heads_i, heads.rearrange("(a r) -> a r", a=1).broadcast_to([NP, ROWS])
                         ).then_inc(heads_in, 16)
            def load_x(j, b):
                after(sp, feat_read, G5 * j + b - G5 + 1)
                sp.dma_start(wide_slot(b)[0:NP, :], x_tiles[j, :, b, :]).then_inc(feat_loaded[b], 16)
            def store_x(j):
                for b in range(G5):
                    sp.wait_ge(xt_kept, G5 * j + b + 1)
                    sp.dma_start(feat_t[0, G5 * j + b], x_turned[:, b, :]).then_inc(x_turned_stored[b], 16)
                    if j + 1 < G5:
                        load_x(j + 1, b)
            load_x(0, 0)
            sp.dma_start(wn[:, :, :], neigh_w[0]).then_inc(wn_in, 16)
            for b in range(1, G5):
                load_x(0, b)
            sp.dma_start(bias_t[:, :, :], bias_cols).then_inc(bias_in, 16)
            sp.dma_start(ws[:, :, :], self_w[0]).then_inc(ws_in, 16)
            for j in range(G5):
                store_x(j)

            def store_h(layer, tile):
                q = tile % G5 % SLOTS
                sp.wait_ge(ht_kept, NT * layer + tile + 1)
                sp.dma_start(feat_t[layer + 1, tile], feat_out[:, q, 0:KT * NP]).then_inc(feat_stored[q], 16)

            def store_out(tile):
                j, b = divmod(tile, G5)
                sp.wait_ge(res_ok, tile + 1)
                sp.dma_start(out_tiles[j, :, b, :], res_sb[:, b % 2, :]).then_inc(out_stored[b % 2], 16)

            def load_features(layer, n):
                def load(j):
                    if n == 1:
                        for q in range(G5 if j == 0 else 0):
                            sp.wait_ge(x_turned_stored[q], 16 * G5)
                    elif n % 2 == 0:
                        for q in range(SLOTS):
                            sp.wait_ge(feat_stored[q], 16 * per_row[q] * (G5 * (layer - 1) + j + 1))
                    for b in range(G5):
                        q, slot = b % SLOTS, feat_in[:, b % SLOTS, :]
                        if n % 2 == 0:
                            q, slot = b, wide_slot(b)
                            if j > 0:
                                sp.wait_ge(feat_read, NT * n + G5 * (j - 1) + b + 1)
                            elif b < SLOTS:
                                sp.wait_ge(feat_read, NT * n + before(b, G5, SLOTS) + 1)
                            else:
                                out_q = (2, 0)[b - SLOTS]
                                sp.wait_ge(feat_stored[out_q], 16 * per_row[out_q] * G5 * layer)
                        elif j == 0 and b < SLOTS:
                            sp.wait_ge(feat_read, NT * n - G5 + b + 1)
                        else:
                            sp.wait_ge(feat_read, NT * n + G5 * j + before(b, G5, SLOTS) + 1)
                        sp.dma_start(slot[:, 0:KT * NP], feat_t[layer, G5 * j + b]).then_inc(feat_loaded[q], 16)
                        if n % 2 and layer + 1 < LAYERS and G5 * j + b >= 4:
                            store_h(layer, G5 * j + b - 4)
                        if n % 2 == 0 and (j, b) in ((0, 2), (1, 1)):
                            store_h(layer - 1, NT - 2 + j)
                        if n == 5:
                            if j == 0 and b < SLOTS:
                                sp.wait_ge(feat_read, NT * n)
                                sp.wait_ge(feat_stored[b], 16 * per_row[b] * G5 * (LAYERS - 1))
                            after(sp, h_ok, 2 * NT + G5 * j + before(b, G5, SLOTS) + 1)
                            sp.dma_start(feat_out[0:NP, b % SLOTS, :], x_tiles[j, :, b, :]
                                         ).then_inc(x_loaded[b % SLOTS], 16)
                            if G5 * j + b >= 4:
                                store_out(G5 * j + b - 4)
                for j in range(G5):
                    load(j)

            for layer in range(LAYERS):
                if layer:
                    load_features(layer, 2 * layer)
                    sp.wait_ge(feat_read, 2 * NT * layer)
                    sp.dma_start(ws[:, :, :], self_w[layer]).then_inc(ws_in, 16)
                load_features(layer, 2 * layer + 1)
                if layer + 1 < LAYERS:
                    store_h(layer, NT - 4)
                    store_h(layer, NT - 3)
                    sp.wait_ge(feat_read if layer else msg_ok, NT * (2 * layer + 1))
                    sp.dma_start(wn[:, :, :], neigh_w[layer + 1]).then_inc(wn_in, 16)
            for tile in range(NT - 4, NT):
                store_out(tile)

        @block.gpsimd
        def _(pool):
            nc.gpsimd.memset(ident[:, :], 0.0).then_inc(pool_step, 1)
            nc.gpsimd.iota(thr_i, pattern=[[NG, 5]], base=0, channel_multiplier=G5).then_inc(constants, 1)
            nc.gpsimd.iota(ramp, pattern=[[1, NP], [0, CW]], base=0, channel_multiplier=0,
                           allow_small_or_imprecise_dtypes=True).then_inc(constants, 1)
            pool.wait_ge(pool_step, 1)
            nc.gpsimd.affine_select(out=ident[:, :], in_=ident[:, :], compare_op=ALU.not_equal, fill=1.0,
                                    base=0, pattern=[[-1, 128]], channel_multiplier=1).then_inc(constants, 1)
            nc.gpsimd.memset(squares[:, :], 0.0).then_inc(range_seen, 1)
            nc.gpsimd.memset(square[:, :], 0.0).then_inc(range_seen, 1)

            for t in range(5):
                pool.wait_ge(rows_at, t + 1)
                nc.gpsimd.indirect_dma_start(
                    out=found_i[:, t, :], out_offset=None, in_=dst[0:E].rearrange("(r n) -> r n", n=NP),
                    in_offset=bass.IndirectOffsetOnAxis(ap=row_i[:, t:t + 1], axis=0),
                    bounds_check=ROWS - 1, oob_is_err=False).then_inc(found_in[t], 16)
            for t in range(5):
                pool.wait_ge(windows_at, t + 1)
                nc.gpsimd.indirect_dma_start(
                    out=win_flat[:, t, :], out_offset=None, in_=pairs,
                    in_offset=bass.IndirectOffsetOnAxis(ap=start_i[:, t:t + 1], axis=0),
                    bounds_check=E, oob_is_err=False).then_inc(win_in, 16)
            nc.gpsimd.indirect_dma_start(
                out=win_w[:, :], out_offset=None, in_=ew.rearrange("(n a) -> n a", a=1),
                in_offset=bass.IndirectOffsetOnAxis(ap=start_i[:, 0:1], axis=0),
                bounds_check=E, oob_is_err=False).then_inc(win_w_in, 16)

            def see_tile(layer, j, b):
                at = 2 * (NT * layer + G5 * j + b)
                pool.wait_ge(hi_ok, NT * layer + G5 * j + b + 1)
                pool.wait_ge(range_seen, at + 2)
                tile = messages[:, G5 * j + b, 0:D]
                nc.gpsimd.tensor_tensor(square[:, :], tile, tile, ALU.mult).then_inc(range_seen, 1)
                pool.wait_ge(range_seen, at + 3)
                nc.gpsimd.tensor_tensor(squares[:, :], squares[:, :], square[:, :], ALU.add).then_inc(range_seen, 1)

            def see_range(layer):
                def row(j):
                    for b in range(G5):
                        see_tile(layer, j, b)
                rows(pool, row)

            nc.gpsimd.memset(lo_scale, LO).then_inc(pool_step, 1)
            pool.wait_ge(pool_step, 2)
            def low(j):
                for b in range(G5):
                    pool.wait_ge(rest_ok, G5 * j + b + 1)
                    nc.gpsimd.tensor_tensor(messages[:, G5 * j + b, D:2 * D], rest_all[:, G5 * j + b, :], lo_scale,
                                            ALU.mult).then_inc(lo_ok, 1)
            rows(pool, low)
            see_range(0)
            pool.wait_ge(hot_ok, NC_ROW * G5)
            nc.gpsimd.iota(slot_no, pattern=[[1, WIN]], base=1, channel_multiplier=0,
                           allow_small_or_imprecise_dtypes=True).then_inc(late_ok, 1)
            nc.gpsimd.iota(ramp_d, pattern=[[1, D]], base=0, channel_multiplier=0,
                           allow_small_or_imprecise_dtypes=True).then_inc(late_ok, 1)
            pool.dma_start(bias_row, bias[LAYERS - 1:LAYERS, :].broadcast_to([NP, D])).then_inc(bias_row_in, 16)
            see_range(1)

            pool.wait_ge(bias_row_in, 16)

            def add_bias(j):
                for b in range(G5):
                    q = b % SLOTS
                    pool.wait_ge(x_loaded[q], 16 * nth(0, j, b))
                    nc.gpsimd.tensor_tensor(feat_out[0:NP, q, :], feat_out[0:NP, q, :], bias_row,
                                            ALU.add).then_inc(xb_ok, 1)
                    see_tile(2, j, b)
            rows(pool, add_bias)
            pool.wait_ge(range_seen, 2 * NT * LAYERS + 2)
            pool.wait_ge(out_stored[0], 16 * 15)
            pool.wait_ge(out_stored[1], 16 * 10)
            nc.gpsimd.memset(square[:, :], 0.0).then_inc(special_done, 1)

            def general_path():
                nc.gpsimd.iota(g_ramp, pattern=[[1, N]], base=0, channel_multiplier=0,
                               allow_small_or_imprecise_dtypes=True).then_inc(g_const, 1)
                nc.gpsimd.iota(g_part, pattern=[[0, 1]], base=0, channel_multiplier=1).then_inc(g_const, 1)
                nc.gpsimd.memset(g_zero, 0.0).then_inc(g_zeroed, 1)
                pool.wait_ge(g_zeroed, 1)
                nc.gpsimd.memset(g_rows[:, D:D + 1], 1.0).then_inc(g_const, 1)
                nc.gpsimd.memset(g_c[:, 31:32], 0.0).then_inc(g_carried, 1)
                with pool.Fori(0, ROWS) as r:
                    pool.wait_ge(g_w_in, r * 16 + 16)
                    pool.wait_ge(g_idx_ok, r + 1)
                    pool.wait_ge(g_carried, r + 1)
                    nc.gpsimd.tensor_tensor(g_c[:, 31:32], g_zero[:, 0:1], g_zero[:, 0:1], ALU.add
                                            ).then_inc(g_carried, 1)
                    nc.gpsimd.indirect_dma_start(
                        out=g_matrix, out_offset=bass.IndirectOffsetOnAxis(ap=g_idx[:, 0:1], axis=0),
                        in_=g_w, in_offset=None, bounds_check=D * D - 1, oob_is_err=False).then_inc(g_scat, 16)
                for layer in range(LAYERS):
                    with pool.Fori(0, ROWS) as r:
                        pool.wait_ge(g_got, r + (layer * ROWS + 1))
                        pool.wait_ge(g_carried, r + ((layer + 1) * ROWS + 1))
                        nc.gpsimd.tensor_tensor(g_c[:, 31:32], g_zero[:, 0:1], g_zero[:, 0:1], ALU.add
                                                ).then_inc(g_carried, 1)
                        nc.gpsimd.indirect_dma_start(
                            out=g_rows[:, 0:D], out_offset=None, in_=x if layer == 0 else g_feat[layer - 1],
                            in_offset=bass.IndirectOffsetOnAxis(ap=g_idx[:, 0:1], axis=0),
                            bounds_check=N - 1, oob_is_err=False).then_inc(g_hot_rows, 16)
            if_general(pool, general_path)

        @block.tensor
        def _(pe):
            pe.wait_ge(constants, 3)
            pe.wait_ge(wn_in, 16)

            def first_messages(j):
                def message(j, b):
                    j, b = (j - 1, b + G5) if b < 0 else (j, b)
                    pe.wait_ge(xt_kept, G5 * j + b + 1)
                    after(pe, rest_ok, G5 * j + b - G5 + 1)
                    for k in range(KT):
                        ins = nc.tensor.matmul(msg[b][0:NP, 0:D], halves(x_turned[:, b, :])[:, k, :],
                                               wn[:, k, :], start=(k == 0), stop=(k == KT - 1))
                    ins.then_inc(msg_ok, 1)

                for b in range(G5):
                    pe.wait_ge(feat_loaded[b], 16 * loaded(0, j, b))
                    after(pe, xt_kept, G5 * j + before(b, G5, 2) + 1)
                    for k in range(KT):
                        ins = nc.tensor.transpose(turn[b % 2][:, k * NP:(k + 1) * NP],
                                                  wide_slot(b)[0:NP, k * 128:(k + 1) * 128],
                                                  ident[0:NP, 0:NP])
                    ins.then_inc(feat_read, 1)
                    if not (isinstance(j, int) and b == 0):
                        message(j, b - 1)
                return message
            message = first_messages(0)
            with pe.Fori(1, G5) as j:
                first_messages(j)
            message(G5, -1)

            pe.wait_ge(keys_ok, 1)
            pe.wait_ge(rest_ok, NT)
            pe.wait_ge(xt_kept, NT)
            for bank, keys in ((own, vc), (turn, vd)):
                for t in range(5):
                    to = bank[t // 4][:, WIN * (t % 4):WIN * (t % 4) + NP]
                    ins = nc.tensor.transpose(to, keys[:, t, :], ident[0:NP, 0:NP])
            ins.then_inc(keys_turned, 1)
            pe.wait_ge(keys_kept, 4)

            def count(j, b, g):
                k = max(k for k in range(NB_TILE) if BANK_STARTS[k] <= g)
                u, at = b * NB_TILE + k, (g - BANK_STARTS[k]) * NP
                if g in STARTS:
                    pe.wait_ge(hot_ok, NC_ROW * j + b * len(CHUNKS) + STARTS.index(g) + 1)
                if at == 0:
                    after(pe, kept, NB_ROW * j + before(u, NB_ROW, 2) + 1)
                c = max(c for c in range(len(CHUNKS)) if STARTS[c] <= g)
                one = [hot[:, (b * len(CHUNKS) + c) % 2, q, 0:NP * CHUNKS[c]].rearrange(
                    "p (v n) -> p v n", n=CHUNKS[c])[:, :, g - STARTS[c]] for q in range(2)]
                ins = nc.tensor.matmul(built[u % 2][0:NP, at:at + NP], one[0], one[1],
                                       start=True, stop=True)
                if at == (BANKS[k] - 1) * NP:
                    ins.then_inc(summed, 1)

            for b in range(G5):
                for g in range(GT):
                    count(0, b, g)

            def turn_h(layer, j, b):
                t = NT * layer + G5 * j + b
                pe.wait_ge(h_ok, t + 1)
                after(pe, ht_kept, t)
                for k in range(KT):
                    ins = nc.tensor.transpose(turn[0][:, k * NP:(k + 1) * NP],
                                              h_of(layer, b)[:, k * 128:(k + 1) * 128], ident[0:NP, 0:NP])
                ins.then_inc(h_turned, 1)

            def aggregate(layer):
                n = 2 * layer + 1

                def mix_h(j, b):
                    t = G5 * j + b
                    pe.wait_ge(ht_kept, 2 * NT + t + 1)
                    after(pe, out_ok, t)
                    for k in range(KT):
                        ins = nc.tensor.matmul(mix[0:NP, 0:D], ut_sb[:, b % G5 % 2, k, :], w1[:, k, :],
                                               start=(k == 0), stop=(k == KT - 1))
                    ins.then_inc(mixed, 1)

                def turn_edges():
                    pe.wait_ge(edges_ok, 1)
                    for q, window in enumerate((win_w, win_s, win_j)):
                        ins = nc.tensor.transpose(turn[1][:, q * GW:(q + 1) * GW], window[0:GW, :],
                                                  ident[0:GW, 0:GW])
                    ins.then_inc(edges_turned, 1)

                def scatter(g):
                    pe.wait_ge(factor_ok, g + 1)
                    if g == GH:
                        pe.wait_ge(w1_ok, 2)
                    for k, bank in enumerate((mix, turn[1])):
                        columns = bank[:, 0:3 * 5 * GH].rearrange("p (q c) -> p q c", q=3)
                        ins = nc.tensor.matmul(columns[:, :, 5 * (g % GH):5 * (g % GH) + 5], factor[:, g % 2, k * 128:(k + 1) * 128],
                                               parts[:, :, g, :], start=True, stop=True)
                    ins.then_inc(scattered, 1)

                def row(j, build=False, edges=False, scattering=False):
                    for b in range(G5):
                        tile = NT * layer + G5 * j + b
                        lagged = not (isinstance(j, int) and j == 0 and b == 0)
                        read, base = (own_read, 0) if layer == 2 else (h_ok, NT * layer)
                        after(pe, read, base + G5 * j + before(b, G5, 3) + 1)
                        if build:
                            pe.wait_ge(kept, NB_ROW * (j + 1))
                        g = 0
                        for q in range(NT):
                            if not lagged and q in (0, 4):
                                pe.wait_ge(lo_ok, NT * (layer + 1) - (3 if q == 0 else 0))
                            ins = nc.tensor.matmul(agg[b % 3][0:NP, :], counts[:, G5 * q + b, bass.ds(j * NP, NP)],
                                                   messages[:, q, :], start=(q == 0), stop=(q == NT - 1))
                            if q == NT - 1:
                                ins.then_inc(agg_ok, 1)
                            if q == (9 if b == 0 else 6):
                                pe.wait_ge(feat_loaded[b % SLOTS], 16 * loaded(n, j, b))
                                after(pe, read, base + G5 * j + before(b, G5, 2) + 1)
                                for k in range(KT):
                                    ins = nc.tensor.matmul(own[b % 2][0:NP, 0:D],
                                                           halves(feat_in[:, b % SLOTS, :])[:, k, :],
                                                           ws[:, k, :], start=(k == 0), stop=(k == KT - 1))
                                ins.then_inc(feat_read, 1)
                            if q == (18 if layer == 2 else 12) and lagged:
                                turn_h(layer, j, b - 1)
                            if q == 10 and layer == 2 and not (isinstance(j, int) and j == 0 and b < 2):
                                mix_h(j, b - 2)
                            if q == 16 and edges and b == 0:
                                turn_edges()
                            if scattering and q >= 10 and q % 2 == 0 and (q - 10) // 2 < GS:
                                first = (G5 * j + b - SCATTER_FROM) * GS
                                if first >= 0:
                                    scatter(first + (q - 10) // 2)
                            while build and g < GT and g * BUILD_SUMS < (q + 1) * GT:
                                count(j + 1, b, g)
                                g += 1

                pe.wait_ge(ws_in, 16 * (layer + 1))
                if layer == 0:
                    row(0, build=True)
                    with pe.Fori(1, G5 - 1) as j:
                        row(j, build=True)
                    pe.wait_ge(kept, NB_ROW * G5)
                    row(G5 - 1)
                elif layer == 1:
                    row(0)
                    with pe.Fori(1, 3) as j:
                        row(j)
                    row(3, edges=True, scattering=True)
                    row(4, scattering=True)
                else:
                    rows(pe, row)
                if layer == 2:
                    mix_h(G5, -2)
                    turn_h(2, G5, -1)
                    mix_h(G5, -1)
                    pe.wait_ge(checks_ok, 1)
                    nc.tensor.matmul(turn[1][0:1, 0:2], small[:, 45:46], small[:, 43:45], start=True, stop=True
                                     ).then_inc(checked, 1)

            def messages_of(layer):
                n = 2 * layer
                pe.wait_ge(wn_in, 16 * (layer + 1))

                def row(j):
                    first = isinstance(j, int) and j == 0
                    for b in range(G5):
                        if first and b == 0:
                            pe.wait_ge(h_ok, NT * layer - 1)
                        if first and b == 3:
                            turn_h(layer - 1, G5, -1)
                        pe.wait_ge(feat_loaded[b], 16 * loaded(n, j, b))
                        after(pe, rest_ok, NT * layer + G5 * (j - 1) + b + 1)
                        for k in range(KT):
                            ins = nc.tensor.matmul(msg[b][0:NP, 0:D], halves(wide_slot(b))[:, k, :],
                                                   wn[:, k, :], start=(k == 0), stop=(k == KT - 1))
                        ins.then_inc(feat_read, 1)
                rows(pe, row)

            aggregate(0)
            messages_of(1)
            aggregate(1)
            messages_of(2)
            pe.wait_ge(w1_ok, 4)
            aggregate(2)

            def general_path():
                pe.wait_ge(g_const, 3)
                with pe.Fori(0, ROWS) as r:
                    pe.wait_ge(g_key_ok, r + 1)
                    nc.tensor.transpose(turn[0][0:NP, 0:NP], g_keys, ident[0:NP, 0:NP]).then_inc(g_keys_t, 1)
                pe.wait_ge(g_in, 32)
                banks = agg + own + turn + [mix]
                for layer in range(LAYERS):
                    with pe.Fori(0, ROWS) as r:
                        pe.wait_ge(g_hot_rows, r * 16 + 16 * (layer * ROWS + 1))
                        pe.wait_ge(g_hot_ok, r + (layer * ROWS + 1))
                        for t in range(NT):
                            if t >= len(banks):
                                pe.wait_ge(g_added, r * NT + (layer * ROWS * NT + t - len(banks) + 1))
                            nc.tensor.matmul(banks[t % len(banks)][0:NP, 0:D + 1], g_hot[:, t * NP:(t + 1) * NP],
                                             g_rows, start=True, stop=True).then_inc(g_summed, 1)
                    pe.wait_ge(g_in, 32 + 32 * (layer + 1))
                    with pe.Fori(0, NT) as t:
                        at = t + (NT * layer + 1)
                        pe.wait_ge(g_tile_in, at * 32)
                        pe.wait_ge(g_mean_ok, at)
                        for q, side in enumerate((g_h, g_mean)):
                            for k in range(KT):
                                ins = nc.tensor.transpose(agg[0][:, (2 * q + k) * NP:(2 * q + k + 1) * NP],
                                                          side[:, k * 128:(k + 1) * 128], ident[0:NP, 0:NP])
                        ins.then_inc(g_turned, 1)
                        pe.wait_ge(g_kept, at if layer < 2 else t * 2 + (2 * NT + 1))
                        for q in range(4):
                            ins = nc.tensor.matmul(own[0][0:NP, 0:D], g_t[:, q, :], (ws, wn)[q // 2][:, q % 2, :],
                                                   start=(q == 0), stop=(q == 3))
                        ins.then_inc(g_prod, 1)
                        if layer == 2:
                            pe.wait_ge(g_unit, t + 1)
                            for k in range(KT):
                                ins = nc.tensor.transpose(agg[0][:, k * NP:(k + 1) * NP],
                                                          g_mean[:, k * 128:(k + 1) * 128], ident[0:NP, 0:NP])
                            ins.then_inc(g_turned, 1)
                            pe.wait_ge(g_kept, t * 2 + (2 * NT + 2))
                            for k in range(KT):
                                ins = nc.tensor.matmul(own[1][0:NP, 0:D], g_t[:, k, :], w1[:, k, :],
                                                       start=(k == 0), stop=(k == 1))
                            ins.then_inc(g_prod, 1)
            if_general(pe, general_path)

        @block.scalar
        def _(act):
            act.dma_start(rows_a, dst[0:E].rearrange("(p n) -> p n", n=ROWS)).then_inc(rows_in, 16)
            act.dma_start(rows_b, dst[1:E + 1].rearrange("(p n) -> p n", n=ROWS)).then_inc(rows_in, 16)
            def hi_of(layer, j, b):
                nc.scalar.activation(messages[:, G5 * j + b, 0:D], msg[b][0:NP, 0:D], ACT.Copy).then_inc(hi_ok, 1)

            def first_row(j):
                def hi(j, b):
                    j, b = (j - 1, b + G5) if b < 0 else (j, b)
                    act.wait_ge(msg_ok, G5 * j + b + 1)
                    hi_of(0, j, b)

                for b in range(G5):
                    tile = G5 * j + b
                    act.wait_ge(feat_read, tile + 1)
                    after(act, x_turned_stored[b], 16 * j)
                    after(act, msg_ok, tile - G5 + 1)
                    nc.scalar.activation(x_turned[:, b, :], turn[b % 2][:, 0:KT * NP],
                                         ACT.Copy).then_inc(xt_kept, 1)
                    if not (isinstance(j, int) and b == 0):
                        hi(j, b - 1)
                return hi
            hi = first_row(0)
            with act.Fori(1, G5) as j:
                first_row(j)
            hi(G5, -1)
            act.wait_ge(keys_turned, 1)
            for bank, keys in ((own, key_src), (turn, key_dst)):
                nc.scalar.activation(keys[:, 0:4 * NP].rearrange("p (t g) -> p t g", t=4),
                                     bank[0][:, :].rearrange("p (t g) -> p t g", g=WIN)[:, :, 0:NP],
                                     ACT.Copy).then_inc(keys_kept, 1)
                nc.scalar.activation(keys[:, 4 * NP:NG], bank[1][:, 0:NP], ACT.Copy).then_inc(keys_kept, 1)
            act.wait_ge(bias_in, 16)
            act.wait_ge(win_w_in, 16)
            act.wait_ge(lo_ok, NT)
            for b in range(G5):
                act.wait_ge(x_turned_stored[b], 16 * G5)

            def keep_counts(j, b, units):
                for u in units:
                    m = BANKS[u]
                    act.wait_ge(summed, NB_ROW * j + b * NB_TILE + u + 1)
                    nc.scalar.activation(counts[:, :, bass.ds(j * NP + b * GT + BANK_STARTS[u], m)],
                                         built[u % 2][0:NP, 0:m * NP].rearrange(
                                             "p (m k) -> p k m", m=m), ACT.Copy).then_inc(kept, 1)
            for b in range(G5):
                keep_counts(0, b, range(NB_TILE))

            def keep_h(layer, j, b):
                j, b = (j - 1, b + G5) if b < 0 else (j, b)
                q, t = b % SLOTS, NT * layer + G5 * j + b
                act.wait_ge(h_turned, t + 1)
                after(act, feat_stored[q], 16 * (nth(layer, j, b) - 1))
                for k in range(KT):
                    ins = nc.scalar.activation(out_slot(q)[:, k, :], turn[0][:, k * NP:(k + 1) * NP], ACT.Relu,
                                               bias=bias_t[:, layer, k:k + 1])
                ins.then_inc(ht_kept, 1)

            def keep_both(j):
                for b in range(G5):
                    if not (isinstance(j, int) and b == 0):
                        keep_counts(j + 1, b, range(EARLY_BANKS))
                        keep_h(0, j, b - 1)
                        keep_counts(j + 1, b, range(EARLY_BANKS, NB_TILE))
                    else:
                        keep_counts(j + 1, b, range(NB_TILE))
            keep_both(0)
            with act.Fori(1, G5 - 1) as j:
                keep_both(j)
            for b in range(G5):
                keep_h(0, G5 - 1, b - 1)

            def keep_hi(layer):
                act.wait_ge(agg_ok, NT * layer)
                act.wait_ge(range_seen, 2 * NT * layer + 2)

                def row(j):
                    for b in range(G5):
                        act.wait_ge(feat_read, 2 * NT * layer + G5 * j + b + 1)
                        hi_of(layer, j, b)
                        if isinstance(j, int) and b == 2:
                            keep_h(layer - 1, G5, -1)
                rows(act, row)

            keep_hi(1)

            def keep_row(j):
                for b in range(G5):
                    if not (isinstance(j, int) and j == 0 and b == 0):
                        keep_h(1, j, b - 1)
            keep_row(0)
            with act.Fori(1, 3) as j:
                keep_row(j)
            act.wait_ge(edges_turned, 1)
            nc.scalar.activation(turned, turn[1][:, 0:3 * GW].rearrange("p (q g) -> p q g", q=3),
                                 ACT.Copy).then_inc(edges_kept, 1)
            keep_row(3)
            keep_row(4)
            keep_hi(2)

            def root(to, at, ok, count):
                act.wait_ge(ok, count)
                nc.scalar.activation(small[:, at + 1:at + 2], small[:, at:at + 1], ACT.Sqrt, bias=small[:, 40:41]
                                     ).then_inc(to, 1)

            def row(j):
                for b in range(G5):
                    t = G5 * j + b
                    root(root_ok, 7, var_ok, t + 1)
                    act.wait_ge(h_turned, 2 * NT + t + 1)
                    after(act, mixed, G5 * j + before(b, G5, 2) + 1)
                    nc.scalar.activation(ut_sb[:, b % 2, :, :],
                                         turn[0][:, 0:KT * NP].rearrange("p (k n) -> p k n", k=KT),
                                         ACT.Copy).then_inc(ht_kept, 1)
                    if not (isinstance(j, int) and b == 0):
                        root(root2_ok, 19, var2_ok, t)
            rows(act, row)
            root(root2_ok, 19, var2_ok, NT)

            def general_path():
                act.dma_start(g_bias, bias.rearrange("(a l) d -> a (l d)", a=1).broadcast_to([NP, LAYERS * D])
                              ).then_inc(g_in, 16)
                act.wait_ge(g_zeroed, 1)
                for half in range(2):
                    act.dma_start(g_matrix.rearrange("(p n) a -> p (n a)", n=1024)[:, half * 512:half * 512 + 512],
                                  g_zero[0:64, :]).then_inc(g_cleared, 16)
                act.wait_ge(g_cleared, 32)
                with act.Fori(0, ROWS) as r:
                    act.dma_start(g_pair, pairs[bass.ds(r * NP, NP), :]).then_inc(g_pair_in, 16)
                    act.dma_start(g_w, ew[bass.ds(r * NP, NP)].rearrange("(p a) -> p a", a=1)).then_inc(g_w_in, 16)
                    act.wait_ge(g_scat, r * 16 + 16)
                act.dma_start(w1, g_matrix.rearrange("(k p n) a -> p k (n a)", k=KT, p=128)).then_inc(g_in, 16)
                for layer in range(LAYERS):
                    with act.Fori(0, ROWS) as r:
                        act.dma_start(g_pair, pairs[bass.ds(r * NP, NP), :]).then_inc(g_pair_in, 16)
                        act.wait_ge(g_added, (r + (layer * ROWS + 1)) * NT)
                    act.dma_start(wn[:, :, :], neigh_w[layer]).then_inc(g_in, 16)
                    act.dma_start(ws[:, :, :], self_w[layer]).then_inc(g_in, 16)
                    feat = x if layer == 0 else g_feat[layer - 1]
                    to = out if layer == LAYERS - 1 else g_feat[layer]
                    with act.Fori(0, NT) as t:
                        act.dma_start(g_h, feat[bass.ds(t * NP, NP), :]).then_inc(g_tile_in, 16)
                        act.dma_start(g_x, x[bass.ds(t * NP, NP), :]).then_inc(g_tile_in, 16)
                        for q in range(2 if layer == 2 else 1):
                            act.wait_ge(g_turned, t + (NT * layer + 1) if layer < 2 else t * 2 + (2 * NT + 1 + q))
                            n = 4 if q == 0 else 2
                            nc.scalar.activation(g_t[:, 0:n, :],
                                                 agg[0][:, 0:n * NP].rearrange("p (q n) -> p q n", q=n),
                                                 ACT.Copy).then_inc(g_kept, 1)
                            if layer == 2:
                                act.wait_ge(g_var, t * 2 + (1 + q))
                                nc.scalar.activation(g_c[:, 8:9], g_c[:, 7:8], ACT.Sqrt, bias=small[:, 40:41]
                                                     ).then_inc(g_root, 1)
                        act.wait_ge(g_st_ok, t + (NT * layer + 1))
                        act.dma_start(to[bass.ds(t * NP, NP), :], g_st).then_inc(g_stored, 16)
                        act.wait_ge(g_stored, t * 16 + 16 * (NT * layer + 1))
                act.wait_ge(g_stored, 16 * NT * LAYERS)
            if_general(act, general_path)

        @block.vector
        def _(dve):
            step = Steps(dve, dve_step)
            v = nc.vector
            dve.wait_ge(constants, 3)
            step(v.tensor_copy(thr, thr_i))
            step(v.memset(small[:, 40:41], EPS))
            dve.wait_ge(heads_in, 16)
            step(v.tensor_copy(heads_f, heads_i))
            for t in range(5):
                step(v.tensor_scalar(junk, heads_f, thr[:, t:t + 1], 0.0, ALU.is_lt, ALU.add,
                                     accum_out=cnt[:, t:t + 1]))
                step(v.tensor_scalar(head_row[:, t:t + 1], cnt[:, t:t + 1], 1.0, 0.0, ALU.subtract, ALU.max))
                v.tensor_copy(row_i[:, t:t + 1], head_row[:, t:t + 1]).then_inc(rows_at, 1)
            dve.wait_ge(rows_in, 32)
            step(v.tensor_tensor(junk, rows_a, rows_b, ALU.is_gt))
            step(v.tensor_reduce(small[:, 41:42], junk, AX.X, ALU.max))

            def first_rest(tile):
                dve.wait_ge(hi_ok, tile + 1)
                v.tensor_tensor(rest_all[:, tile, :], msg[tile % G5][0:NP, 0:D], messages[:, tile, 0:D],
                                ALU.subtract).then_inc(rest_ok, 1)

            for t in range(5):
                dve.wait_ge(found_in[t], 16)
                step(v.tensor_copy(found_f[:, t, :], found_i[:, t, :]))
                step(v.tensor_scalar(junk[:, 0:NP], found_f[:, t, :], thr[:, t:t + 1], 0.0, ALU.is_lt, ALU.add,
                                     accum_out=fine[:, t:t + 1]))
                step(v.scalar_tensor_tensor(out=head_row[:, t:t + 1], in0=head_row[:, t:t + 1], scalar=float(NP),
                                            in1=fine[:, t:t + 1], op0=ALU.mult, op1=ALU.add))
                v.tensor_copy(start_i[:, t:t + 1], head_row[:, t:t + 1]).then_inc(windows_at, 1)
                first_rest(t)
            for tile in range(G5, WINDOWS_AT):
                first_rest(tile)
            def split_rows(layer):
                dve.wait_ge(agg_ok, NT * layer)
                dve.wait_ge(h_ok, NT * layer)

                def low(j, b):
                    j, b = (j - 1, b + G5) if b < 0 else (j, b)
                    tile = G5 * j + b
                    dve.wait_ge(rest_ok, NT * layer + tile + 1)
                    v.tensor_scalar(messages[:, tile, D:2 * D], rest_of[b % 3], LO, None, ALU.mult).then_inc(lo_ok, 1)

                def row(j):
                    for b in range(G5):
                        tile = G5 * j + b
                        dve.wait_ge(hi_ok, NT * layer + tile + 1)
                        after(dve, lo_ok, NT * layer + G5 * j + before(b, G5, 3) + 1)
                        v.tensor_tensor(rest_of[b % 3], msg[b][0:NP, 0:D], messages[:, tile, 0:D],
                                        ALU.subtract).then_inc(rest_ok, 1)
                        if not (isinstance(j, int) and b == 0):
                            low(j, b - 1)
                rows(dve, row)
                low(G5, -1)
            tile = WINDOWS_AT - 1
            dve.wait_ge(win_in, 80)
            step(v.tensor_copy(f_src, win[:, :, :, 1]))
            first_rest(tile := tile + 1)
            step(v.tensor_tensor(jd, win[:, :, :, 0], thr.unsqueeze(2).broadcast_to([NP, 5, WIN]), ALU.subtract))
            first_rest(tile := tile + 1)
            step(v.tensor_scalar(va, jd, 0.0, None, ALU.is_ge))
            first_rest(tile := tile + 1)
            step(v.scalar_tensor_tensor(out=va, in0=jd, scalar=4.0, in1=va, op0=ALU.is_le, op1=ALU.mult))
            first_rest(tile := tile + 1)
            step(v.tensor_scalar(vb, f_src, 1.0 / NG, -0.4992, ALU.mult, ALU.add))
            first_rest(tile := tile + 1)
            step(v.tensor_scalar(vb, vb, MAGIC, None, ALU.add))
            first_rest(tile := tile + 1)
            step(v.tensor_scalar(vb, vb, MAGIC, None, ALU.subtract))
            first_rest(tile := tile + 1)
            step(v.scalar_tensor_tensor(out=src, in0=vb, scalar=-float(NG), in1=f_src, op0=ALU.mult, op1=ALU.add))
            first_rest(tile := tile + 1)
            step(v.tensor_scalar(vc, src, 1.0 / G5, -0.4, ALU.mult, ALU.add))
            first_rest(tile := tile + 1)
            step(v.tensor_scalar(vc, vc, MAGIC, None, ALU.add))
            first_rest(tile := tile + 1)
            step(v.tensor_scalar(vc, vc, MAGIC, None, ALU.subtract))
            first_rest(tile := tile + 1)
            step(v.scalar_tensor_tensor(out=vd, in0=vc, scalar=-float(G5), in1=src, op0=ALU.mult, op1=ALU.add))
            first_rest(tile := tile + 1)
            step(v.scalar_tensor_tensor(out=vd, in0=vd, scalar=5.0, in1=jd, op0=ALU.mult, op1=ALU.add))
            first_rest(tile := tile + 1)
            step(v.scalar_tensor_tensor(out=vd, in0=vb, scalar=25.0, in1=vd, op0=ALU.mult, op1=ALU.add))
            first_rest(tile := tile + 1)
            step(v.scalar_tensor_tensor(out=vd, in0=vd, scalar=1.0, in1=va, op0=ALU.add, op1=ALU.mult))
            first_rest(tile := tile + 1)
            v.tensor_scalar(vd, vd, 1.0, None, ALU.subtract).then_inc(keys_ok, 1)
            step(v.scalar_tensor_tensor(out=slot_j, in0=jd, scalar=1.0, in1=va, op0=ALU.add, op1=ALU.mult))
            step(v.tensor_copy(win_s[:, :], f_src[:, 0, :]))
            step(v.tensor_scalar(win_j[:, :], slot_j[:, 0, :], 1.0, None, ALU.subtract))

            def degree_of(t, j):
                step(v.tensor_scalar(no_use, slot_j[:, t, :], float(j + 1), 0.0, ALU.is_equal, ALU.add,
                                     accum_out=degree[:, G5 * t + j:G5 * t + j + 1]))

            for t in range(2):
                for j in range(G5):
                    degree_of(t, j)
            dve.wait_ge(keys_kept, 4)

            def make_hot(j, w, degrees=False):
                b, c = divmod(w, len(CHUNKS))
                n = CHUNKS[c]
                after(dve, summed, NB_ROW * j + 2 * (w - 2) + 2)
                for q, keys in enumerate((key_src, key_dst)):
                    ins = v.tensor_tensor(
                        hot[:, w % 2, q, 0:NP * n].rearrange("p (v n) -> p v n", n=n), ramp[:, :, 0:n],
                        keys[:, bass.ds(j * NP + b * GT + STARTS[c], n)].unsqueeze(1).broadcast_to([128, NP, n]),
                        ALU.is_equal)
                ins.then_inc(hot_ok, 1)
                if degrees and w > 1 and w - 2 < 3 * G5:
                    degree_of(2 + (w - 2) // G5, (w - 2) % G5)
            for w in range(NC_ROW):
                make_hot(0, w, degrees=True)
            step(v.tensor_scalar(inv_deg[:, :], degree[:, :], 1.0, None, ALU.max))
            step(v.reciprocal(inv_deg[:, :], inv_deg[:, :]))
            step(v.scalar_tensor_tensor(out=inv_deg[:, :], in0=degree[:, :], scalar=0.0, in1=inv_deg[:, :],
                                        op0=ALU.is_gt, op1=ALU.mult))
            step.done()

            def make_h(layer, j, b):
                t = NT * layer + G5 * j + b
                dve.wait_ge(agg_ok, t + 1)
                agg_sb = rest[:, 0, :]
                step(v.tensor_scalar(agg_sb, agg[b % 3][0:NP, D:2 * D], 1.0 / LO, None, ALU.mult))
                step(v.tensor_tensor(agg_sb, agg_sb, agg[b % 3][0:NP, 0:D], ALU.add))
                after(dve, h_turned, NT * layer + G5 * j + before(b, G5, 2) + 1)
                return v.scalar_tensor_tensor(out=h_of(layer, b), in0=agg_sb,
                                              scalar=inv_deg[:, bass.ds(G5 * j + b, 1)], in1=own[b % 2][0:NP, 0:D],
                                              op0=ALU.mult, op1=ALU.add)

            def row0(j, last=False):
                step.row(j, 2 * G5)
                for b in range(G5):
                    for w in range(4 * b + 2, 4 * b + 6):
                        if w < NC_ROW:
                            make_hot(j + 1, w)
                        elif not last:
                            make_hot(j + 2, w - NC_ROW)
                    make_h(0, j, b).then_inc(h_ok, 1)
            for w in range(2):
                make_hot(1, w)
            row0(0)
            with dve.Fori(1, G5 - 2) as j:
                row0(j)
            row0(G5 - 2, last=True)
            step.row(G5 - 1, 2 * G5)
            for b in range(G5):
                make_h(0, G5 - 1, b).then_inc(h_ok, 1)
            step.end_rows(2 * G5)
            dve.wait_ge(summed, NB_ROW * G5)
            dve.wait_ge(late_ok, 2)
            step(v.memset(win_k, 0.0))
            step(v.tensor_scalar(win_v, win_j[0:GW, :], 0.0, None, ALU.is_ge))
            step(v.scalar_tensor_tensor(out=win_v, in0=win_s[0:GW, :], scalar=float(D), in1=win_v,
                                        op0=ALU.is_lt, op1=ALU.mult))
            step(v.scalar_tensor_tensor(out=win_q, in0=win_s[0:GW, :], scalar=5.0, in1=win_j[0:GW, :],
                                        op0=ALU.mult, op1=ALU.add))
            step(v.scalar_tensor_tensor(out=win_k[:, 0:WIN], in0=win_q, scalar=1.0, in1=win_v,
                                        op0=ALU.add, op1=ALU.mult))
            step.done()
            split_rows(1)

            def last_use(i):
                mine = win_k[:, bass.ds(i, NL)].unsqueeze(2).broadcast_to([GW, NL, WIN])
                theirs = win_k[:, 0:WIN].unsqueeze(1).broadcast_to([GW, NL, WIN])
                step(v.tensor_tensor(same, mine, theirs, ALU.is_equal))
                step(v.tensor_tensor(same, same, slot_no.unsqueeze(1).broadcast_to([GW, NL, WIN]), ALU.mult))
                step(v.tensor_reduce(last[:, bass.ds(i, NL)], same, AX.X, ALU.max))

            def make_factor(g):
                after(dve, scattered, g - 1)
                v.tensor_scalar(factor[:, g % 2, :], ramp_d, turned[:, 1, g:g + 1], None,
                                ALU.is_equal).then_inc(factor_ok, 1)

            def row1(j):
                step.row(j, 5 * G5)
                for b in range(G5):
                    last_use((G5 * j + b) * NL)
                    make_h(1, j, b).then_inc(h_ok, 1)
            row1(0)
            with dve.Fori(1, 3) as j:
                row1(j)
            step.base += 3 * 5 * G5
            step.start, step.k = step.base, 0
            step(v.tensor_tensor(last[:, 0:WIN], last[:, 0:WIN], slot_no, ALU.is_equal))
            step(v.scalar_tensor_tensor(out=last[:, 0:WIN], in0=win_k[:, 0:WIN], scalar=0.5, in1=last[:, 0:WIN],
                                        op0=ALU.is_gt, op1=ALU.mult))
            dve.wait_ge(win_w_in, 16)
            v.tensor_tensor(win_w[0:GW, :], win_w[0:GW, :], last[:, 0:WIN], ALU.mult).then_inc(edges_ok, 1)
            def join_parts(half):
                dve.wait_ge(scattered, GH * (half + 1))
                n = min(5 * GH, D - half * 5 * GH)
                for k, bank in enumerate((mix, turn[1])):
                    v.tensor_reduce(w1[:, k, bass.ds(half * 5 * GH, n)],
                                    bank[:, 0:3 * 5 * GH].rearrange("p (q c) -> p c q", q=3)[:, 0:n, :],
                                    AX.X, ALU.add).then_inc(w1_ok, 1)

            for t in range(3 * G5, NT):
                if t == 3 * G5 + 1:
                    dve.wait_ge(edges_kept, 1)
                    for j in range(5):
                        ins = v.tensor_scalar(hot_j[:, :, j], turned[:, 2, :], float(j), None, ALU.is_equal)
                    step(ins)
                    for q in range(3):
                        step(v.tensor_copy(part, turned[:, 0, :]))
                        step(v.tensor_tensor(parts[:, q], hot_j,
                                             part.unsqueeze(2).broadcast_to([128, GW, 5]), ALU.mult))
                        if q < 2:
                            step(v.tensor_tensor(turned[:, 0, :], turned[:, 0, :], part, ALU.subtract))
                first = (t - SCATTER_FROM) * GS
                if first == GH:
                    join_parts(0)
                if 0 <= first < GW:
                    for g in range(first, first + GS):
                        make_factor(g)
                make_h(1, t // G5, t % G5).then_inc(h_ok, 1)
            join_parts(1)
            step.done()
            split_rows(2)
            def norm(value, at, t, var, root):
                step(v.bn_stats(small[:, at:at + 6], value))
                v.memset(small[:, 60:61], 0.0)
                v.bn_aggr(small[:, at + 6:at + 8], small[:, at:at + 6]).then_inc(var, 1)
                dve.wait_ge(root, t + 1)
                step(v.reciprocal(small[:, at + 9:at + 10], small[:, at + 8:at + 9]))

            def nth2(j, b):
                return (3, 2)[b % 2] * j + b // 2 + 1

            def finish(j, b):
                j, b = (j - 1, b + G5) if b < 0 else (j, b)
                t = G5 * j + b
                r = res_sb[:, b % 2, :]
                dve.wait_ge(mixed, t + 1)
                after(dve, out_stored[b % 2], 16 * (nth2(j, b) - 1))
                v.tensor_tensor(r, h_of(2, b), mix[0:NP, 0:D], ALU.add).then_inc(out_ok, 1)
                dve.wait_ge(out_ok, t + 1)
                norm(r, 12, t, var2_ok, root2_ok)
                v.tensor_scalar(r, r, small[:, 18:19], small[:, 21:22], ALU.subtract, ALU.mult).then_inc(res_ok, 1)

            def row2(j):
                step.row(j, 7 * G5)
                if not isinstance(j, int):
                    step.start = step.start - 2
                for b in range(G5):
                    t = G5 * j + b
                    make_h(2, j, b).then_inc(own_read, 1)
                    dve.wait_ge(own_read, t + 1)
                    z = h_of(2, b)
                    dve.wait_ge(xb_ok, t + 1)
                    step(v.tensor_tensor(z, z, feat_out[0:NP, b % SLOTS, :], ALU.add))
                    norm(z, 0, t, var_ok, root_ok)
                    v.tensor_scalar(z, z, small[:, 6:7], small[:, 9:10], ALU.subtract, ALU.mult).then_inc(h_ok, 1)
                    if not (isinstance(j, int) and b == 0):
                        finish(j, b - 1)
            row2(0)
            with dve.Fori(1, G5) as j:
                row2(j)
            step.base, step.k = step.base + 5 * 7 * G5 - 2, 0
            step.start = step.base
            finish(G5, -1)
            dve.wait_ge(range_seen, 2 * NT * LAYERS + 2)
            step(v.tensor_reduce(small[:, 42:43], squares[:, :], AX.X, ALU.add))
            step(v.tensor_scalar(small[:, 42:43], small[:, 42:43], HI_MAX * HI_MAX, None, ALU.is_lt))
            step(v.scalar_tensor_tensor(out=small[:, 43:44], in0=small[:, 41:42], scalar=1.0,
                                        in1=small[:, 42:43], op0=ALU.add, op1=ALU.subtract))
            step(v.tensor_reduce(small[:, 44:45], degree[:, :], AX.X, ALU.add))
            v.memset(small[:, 45:46], 1.0).then_inc(checks_ok, 1)
            dve.wait_ge(checked, 1)
            step(v.tensor_scalar(small[0:1, 46:47], turn[1][0:1, 1:2], float(E), None, ALU.not_equal))
            step(v.tensor_scalar(small[0:1, 47:48], turn[1][0:1, 0:1], 0.0, None, ALU.is_gt))
            step(v.tensor_tensor(small[0:1, 46:47], small[0:1, 46:47], small[0:1, 47:48], ALU.max))
            v.tensor_copy(general[0:1, 0:1], small[0:1, 46:47]).then_inc(general_ok, 1)

            def general_path():
                dve.wait_ge(g_const, 3)
                one = Steps(dve, g_step)
                one(v.tensor_copy(g_c[:, 0:1], g_part))
                one(v.tensor_scalar(g_later, g_ramp[:, 0:NP], g_c[:, 0:1], None, ALU.is_gt))
                one.done()
                per = 7
                with dve.Fori(0, ROWS) as r:
                    one.row(r, per)
                    dve.wait_ge(g_pair_in, r * 16 + 16)
                    one(v.tensor_copy(g_c[:, 1:3], g_pair))
                    one(v.tensor_scalar(g_c[:, 3:5], g_c[:, 1:3], float(D), None, ALU.is_lt))
                    one(v.tensor_tensor(g_c[:, 3:4], g_c[:, 3:4], g_c[:, 4:5], ALU.mult))
                    one(v.scalar_tensor_tensor(out=g_c[:, 5:6], in0=g_c[:, 2:3], scalar=float(D), in1=g_c[:, 1:2],
                                               op0=ALU.mult, op1=ALU.add))
                    one(v.scalar_tensor_tensor(out=g_c[:, 5:6], in0=g_c[:, 5:6], scalar=-float(D * D),
                                               in1=g_c[:, 3:4], op0=ALU.add, op1=ALU.mult))
                    v.tensor_scalar(g_keys, g_zero[:, 0:NP], g_c[:, 5:6], None, ALU.add).then_inc(g_key_ok, 1)
                    dve.wait_ge(g_keys_t, r + 1)
                    one(v.scalar_tensor_tensor(out=g_same, in0=turn[0][0:NP, 0:NP], scalar=g_c[:, 5:6], in1=g_later,
                                               op0=ALU.is_equal, op1=ALU.mult))
                    one(v.tensor_reduce(g_c[:, 6:7], g_same, AX.X, ALU.max))
                    v.scalar_tensor_tensor(out=g_c[:, 10:11], in0=g_c[:, 6:7], scalar=float(D * D), in1=g_c[:, 5:6],
                                           op0=ALU.mult, op1=ALU.add).then_inc(g_step2, 1)
                    dve.wait_ge(g_step2, r + 1)
                    v.tensor_scalar(g_idx, g_c[:, 10:11], float(D * D), None, ALU.add).then_inc(g_idx_ok, 1)
                assert one.k == per
                one.base += ROWS * per
                one.start, one.k = one.base, 0
                dve.wait_ge(g_in, 32)

                def general_norm(value, t, q):
                    one(v.bn_stats(g_c[:, 12:18], value))
                    v.memset(g_c[:, 30:31], 0.0)
                    v.bn_aggr(g_c[:, 6:8], g_c[:, 12:18]).then_inc(g_var, 1)
                    dve.wait_ge(g_root, t * 2 + (1 + q))
                    one(v.reciprocal(g_c[:, 9:10], g_c[:, 8:9]))

                for layer in range(LAYERS):
                    one(v.memset(g_sum, 0.0))
                    one.done()
                    with dve.Fori(0, ROWS) as r:
                        one.row(r, 1)
                        dve.wait_ge(g_pair_in, r * 16 + 16 * ((layer + 1) * ROWS + 1))
                        v.tensor_copy(g_idx, g_pair[:, 1:2]).then_inc(g_got, 1)
                        one(v.tensor_copy(g_c[:, 1:2], g_pair[:, 0:1]))
                        v.tensor_scalar(g_hot, g_ramp, g_c[:, 1:2], None, ALU.is_equal).then_inc(g_hot_ok, 1)
                        banks = agg + own + turn + [mix]
                        for t in range(NT):
                            dve.wait_ge(g_summed, r * NT + (layer * ROWS * NT + t + 1))
                            v.tensor_tensor(g_sum[:, t, :], g_sum[:, t, :], banks[t % len(banks)][0:NP, 0:D + 1],
                                            ALU.add).then_inc(g_added, 1)
                    one.base += ROWS
                    one.start, one.k = one.base, 0
                    dve.wait_ge(g_added, (layer + 1) * ROWS * NT)
                    per = 3 if layer < 2 else 9
                    with dve.Fori(0, NT) as t:
                        one.row(t, per)
                        at = t + (NT * layer + 1)
                        degrees = g_sum[:, t, D:D + 1]
                        one(v.tensor_scalar(g_c[:, 2:3], degrees, 1.0, None, ALU.max))
                        one(v.reciprocal(g_c[:, 3:4], g_c[:, 2:3]))
                        v.tensor_scalar(g_mean, g_sum[:, t, 0:D], g_c[:, 3:4], None, ALU.mult).then_inc(g_mean_ok, 1)
                        dve.wait_ge(g_prod, at if layer < 2 else t * 2 + (2 * NT + 1))
                        one(v.tensor_tensor(g_st, own[0][0:NP, 0:D], g_bias[:, layer * D:(layer + 1) * D], ALU.add))
                        if layer < 2:
                            v.tensor_scalar(g_st, g_st, 0.0, None, ALU.max).then_inc(g_st_ok, 1)
                        else:
                            dve.wait_ge(g_tile_in, at * 32)
                            one(v.tensor_tensor(g_st, g_st, g_x, ALU.add))
                            general_norm(g_st, t, 0)
                            v.tensor_scalar(g_mean, g_st, g_c[:, 6:7], g_c[:, 9:10], ALU.subtract, ALU.mult
                                            ).then_inc(g_unit, 1)
                            dve.wait_ge(g_prod, t * 2 + (2 * NT + 2))
                            one(v.tensor_tensor(g_st, g_mean, own[1][0:NP, 0:D], ALU.add))
                            general_norm(g_st, t, 1)
                            v.tensor_scalar(g_st, g_st, g_c[:, 6:7], g_c[:, 9:10], ALU.subtract, ALU.mult
                                            ).then_inc(g_st_ok, 1)
                    assert one.k == per, (one.k, per)
                    one.base += NT * per
                    one.start, one.k = one.base, 0
            if_general(dve, general_path)


_OUT = (N, D)


def kernel(x, src, dst, edge_weight, L0_gnn_W_self, L0_gnn_W_neigh, L0_gnn_bias):
    import numpy as np
    import concourse.bacc as bacc
    from concourse.bass_utils import run_bass_kernel_spmd as run

    src, dst, ew = np.asarray(src), np.asarray(dst), np.asarray(edge_weight)
    dst_pad = np.concatenate([dst, np.full(WIN, N, dst.dtype)])
    src_pad = np.concatenate([src, np.zeros(WIN, src.dtype)])
    arrays = {
        "x": np.asarray(x),
        "pairs": np.ascontiguousarray(np.stack([dst_pad, src_pad], 1)),
        "dst": dst_pad,
        "heads": np.ascontiguousarray(dst[::NP]),
        "ew": np.concatenate([ew, np.zeros(WIN, ew.dtype)]),
        "w_self": np.asarray(L0_gnn_W_self),
        "w_neigh": np.asarray(L0_gnn_W_neigh),
        "bias": np.asarray(L0_gnn_bias),
        "bias_cols": np.ascontiguousarray(np.asarray(L0_gnn_bias).reshape(LAYERS, KT, 128).transpose(2, 0, 1)),
    }
    nc = bacc.Bacc("TRN2", target_bir_lowering=False, num_devices=1)
    args = [nc.dram_tensor(k, v.shape, mybir.dt.from_np(v.dtype), kind="ExternalInput").ap()
            for k, v in arrays.items()]
    out = nc.dram_tensor("out", _OUT, F32, kind="ExternalOutput").ap()
    feat_t = nc.dram_tensor("feat_t", (LAYERS, NT, 128, KT * NP), F32, kind="Internal").ap()
    g_feat = [nc.dram_tensor(f"g_feat{q}", (N, D), F32, kind="Internal").ap() for q in range(LAYERS - 1)]
    g_matrix = nc.dram_tensor("g_matrix", (D * D, 1), F32, kind="Internal").ap()
    build(nc, *args, out, feat_t, g_feat, g_matrix)
    return run(nc, [arrays], core_ids=[0]).results[0]["out"]
```
